# Optimizing a Trainium2 kernel written in Bass

```python
import numpy as np
import jax
import jax.numpy as jnp

def _softmax(x, axis=-1):
    return jax.nn.softmax(x, axis=axis)
def _gelu(x):
    return jax.nn.gelu(x, approximate=True)
def _silu(x):
    return jax.nn.silu(x)
def _sigmoid(x):
    return jax.nn.sigmoid(x)
def _layernorm(x, axis=-1, eps=1e-5):
    m = jnp.mean(x, axis=axis, keepdims=True)
    v = jnp.var(x, axis=axis, keepdims=True)
    return (x - m) / jnp.sqrt(v + eps)
def _scatter_add(tgt, idx, src, axis=0):
    return tgt.at[idx].add(src)
def _segment_sum(src, seg, n):
    return jax.ops.segment_sum(src, seg, n)

kernel_name = 'mk_adj_resnorm_d1_adj_512_d124f0'

def setup_inputs(seed: int = 0):
    np.random.seed(seed)
    _w = jnp.asarray
    def _rec_inputs():
        import jax
        import jax.numpy as jnp
        _gk = jax.random.key(seed)
        x = -0.0005963 + 1.001 * jax.random.normal(jax.random.fold_in(_gk, 1), (3327, 512), jnp.float32)
        _w = (1.0 + jnp.arange(3327, dtype=jnp.float32)) ** -0.5
        _w = _w / _w.mean()
        _pij = jnp.clip(0.00480914 * _w[:, None] * _w[None, :], 0.0, 1.0)
        _a = jax.random.uniform(jax.random.fold_in(_gk, 2), (3327, 3327)) < _pij
        _af = _a.astype(jnp.float32)
        adj = _af
        return x, adj
    x, adj = _rec_inputs()
    def _L0_gnn_setup():
        import jax, jax.numpy as jnp
        import numpy as np
        N = 6144
        D_IN = 512
        D_OUT = 512
        DENSITY = 0.005
        key = jax.random.key(seed)
        ks = jax.random.split(key, 12)
        x = jax.random.normal(ks[0], (N, D_IN), dtype=jnp.float32)
        adj_a = (jax.random.uniform(ks[1], (N, N)) < DENSITY).astype(jnp.float32)
        adj_b = (jax.random.uniform(ks[2], (N, N)) < DENSITY).astype(jnp.float32)
        W_sa = jax.random.normal(ks[3], (D_IN, D_OUT), dtype=jnp.float32) * (1.414 / np.sqrt(D_IN + D_OUT))
        a_sa = jax.random.normal(ks[4], (1, 2 * D_OUT), dtype=jnp.float32) * (1.414 / np.sqrt(1 + 2 * D_OUT))
        stdv = 1.0 / np.sqrt(D_OUT)
        W_gcnb = jax.random.uniform(ks[5], (D_IN, D_OUT), minval=-stdv, maxval=stdv, dtype=jnp.float32)
        b_gcnb = jax.random.uniform(ks[6], (D_OUT,), minval=-stdv, maxval=stdv, dtype=jnp.float32)
        s = 1.0 / np.sqrt(2 * D_IN)
        Wa = jax.random.uniform(ks[7], (1, 2 * D_IN), minval=-s, maxval=s, dtype=jnp.float32)
        ba = jax.random.uniform(ks[8], (1,), minval=-s, maxval=s, dtype=jnp.float32)
        Wb = jax.random.uniform(ks[9], (1, 2 * D_IN), minval=-s, maxval=s, dtype=jnp.float32)
        bb = jax.random.uniform(ks[10], (1,), minval=-s, maxval=s, dtype=jnp.float32)
        return {'x': x, 'adj_a': adj_a, 'adj_b': adj_b, 'W_sa': W_sa, 'a_sa': a_sa, 'W_gcnb': W_gcnb, 'b_gcnb': b_gcnb, 'Wa': Wa, 'ba': ba, 'Wb': Wb, 'bb': bb}
    _L0_gnn_all = _L0_gnn_setup()
    _L0_gnn_in = {k: v for k, v in _L0_gnn_all.items() if k in ('W_sa', 'a_sa', 'W_gcnb', 'b_gcnb', 'Wa', 'ba', 'Wb', 'bb', )}
    del _L0_gnn_all

    return {
        "x": x,
        "adj": adj,
        "L0_gnn_W_sa": _L0_gnn_in["W_sa"],
        "L0_gnn_a_sa": _L0_gnn_in["a_sa"],
        "L0_gnn_W_gcnb": _L0_gnn_in["W_gcnb"],
        "L0_gnn_b_gcnb": _L0_gnn_in["b_gcnb"],
        "L0_gnn_Wa": _L0_gnn_in["Wa"],
        "L0_gnn_ba": _L0_gnn_in["ba"],
        "L0_gnn_Wb": _L0_gnn_in["Wb"],
        "L0_gnn_bb": _L0_gnn_in["bb"],
    }

def reference(x, adj, L0_gnn_W_sa, L0_gnn_a_sa, L0_gnn_W_gcnb, L0_gnn_b_gcnb, L0_gnn_Wa, L0_gnn_ba, L0_gnn_Wb, L0_gnn_bb):
    import jax
    import jax.numpy as jnp
    def _L0_gnn_ref(x, adj_a, adj_b, W_sa, a_sa, W_gcnb, b_gcnb, Wa, ba, Wb, bb):
        import jax, jax.numpy as jnp
        import numpy as np
        N = 6144
        D_IN = 512
        D_OUT = 512
        DENSITY = 0.005
        type_sum_a = adj_a @ x
        type_sum_b = adj_b @ x
        attn_a = jax.nn.sigmoid(jnp.concatenate([type_sum_a, x], axis=1) @ Wa.T + ba)
        attn_b = jax.nn.sigmoid(jnp.concatenate([type_sum_b, x], axis=1) @ Wb.T + bb)
        h = x @ W_sa
        Hd = h.shape[1]
        s_left = h @ a_sa[0, :Hd]
        s_right = h @ a_sa[0, Hd:]
        scores = s_left[:, None] + s_right[None, :]
        e = jnp.where(adj_a != 0, jnp.exp(-jax.nn.leaky_relu(scores, 0.01)), 0.0)
        attn = e / (jnp.sum(e, axis=1, keepdims=True) + 1e-05)
        x_a = attn @ h
        x_b = adj_b @ (x @ W_gcnb) + b_gcnb
        return jax.nn.sigmoid(attn_a * x_a + attn_b * x_b)

    x = _layernorm(x + _L0_gnn_ref(x, adj, adj, L0_gnn_W_sa, L0_gnn_a_sa, L0_gnn_W_gcnb, L0_gnn_b_gcnb, L0_gnn_Wa, L0_gnn_ba, L0_gnn_Wb, L0_gnn_bb), axis=-1)
    return x


_drawn_inputs = setup_inputs


def setup_inputs(seed=0):
    import zlib

    import numpy as np

    out = dict(_drawn_inputs(seed))
    spreads = {}
    factors = {'L0_gnn_a_sa': 3.283, 'L0_gnn_b_gcnb': 21.63, 'L0_gnn_Wa': 3.196}
    for name, (base, spread) in spreads.items():
        noise = np.random.default_rng([zlib.crc32(name.encode()), seed]).standard_normal(out[name].shape)
        drawn = base * np.exp(spread * noise) if base else spread * noise
        out[name] = jnp.asarray(drawn.astype(out[name].dtype))
    for name, factor in factors.items():
        out[name] = (out[name] * factor).astype(out[name].dtype)
    return out
```

```python
from contextlib import ExitStack

import concourse.bass as bass
from concourse import mybir

ALU = mybir.AluOpType
ACT = mybir.ActivationFunctionType
AX_X = mybir.AxisListType.X
F32 = mybir.dt.float32
F32R = mybir.dt.float32r
BF16 = mybir.dt.bfloat16

P = 128
SLOPE = 0.01
EPS_ATTN = 1e-5
EPS_NORM = 1e-5

RING = 3
E_RING = 2
STAGES = 4


def chunks_of(tiles):
    sizes = [5, 4, 4, 5, 4, 4]
    assert sum(sizes) == tiles and len(sizes) % RING == 0 and len(sizes) % E_RING == 0
    return [(sum(sizes[:c]), n) for c, n in enumerate(sizes)]


def adj_resnorm_kernel(nc, x, adj_t, w_sa, a_sa, w_gcnb, b_gcnb, wa, ba, wb, bb, out):
    TILES, _, D = x.shape
    KT = D // P
    CHUNKS = chunks_of(TILES)
    NC = len(CHUNKS)
    LAST = TILES - 1
    NST = KT + TILES + KT
    assert TILES % 2 == 0

    with ExitStack() as ctx:
        def sb(name, shape, dt=F32):
            return ctx.enter_context(nc.sbuf_tensor(name, shape, dt))

        def psum(name, shape):
            return ctx.enter_context(nc.psum_tensor(name, shape, F32))

        def sem(name):
            return ctx.enter_context(nc.semaphore(name))

        x_hi = sb("x_hi", [P, TILES, D], F32R)
        x_lo = sb("x_lo", [P, TILES, D], F32R)
        w_hi = sb("w_hi", [P, 2, KT, D], F32R)
        w_lo = sb("w_lo", [P, 2, KT, D], F32R)
        width = [CHUNKS[s][1] for s in range(RING)]
        adj = [sb(f"adj{s}", [P, width[s], P]) for s in range(RING)]
        adj_r = [sb(f"adj_r{s}", [P, width[s], P], F32R) for s in range(RING)]
        e_hi = [sb(f"e_hi{s}", [P, width[s], P], F32R) for s in range(RING)]
        e_lo = [sb(f"e_lo{s}", [P, width[s], P], F32R) for s in range(RING)]
        e_raw = [sb(f"e_raw{s}", [P, max(width), P]) for s in range(E_RING)]
        esum = sb("esum", [P, 2, NC, P])
        zt_hi = sb("zt_hi", [P, 2, D], F32R)
        zt_lo = sb("zt_lo", [P, 2, D], F32R)
        work = sb("work", [P, STAGES, D])
        stage = [work[:, n, :] for n in range(STAGES)]
        zs = work[:, 0:2, :]
        y = [work[:, 2, :], work[:, 3, :]]
        x_row = sb("x_row", [P, D])
        product = sb("product", [P, D], BF16)
        a_row = [x_row[:, :], sb("a_right", [P, D])[:, :]]
        v_l = sb("v_l", [P, D])
        v_r = a_row[1]
        w_gate = sb("w_gate", [P, 2, 2, D])
        bias_row = v_r
        ident = sb("ident", [P, P])
        ones = sb("ones", [P, P])
        diag = sb("diag", [P, P])
        l_row = sb("l_row", [P, 2, P])
        r_col = sb("r_col", [P, TILES])
        r_neg = sb("r_neg", [P, TILES])
        v_col = sb("v_col", [P, 2, KT])
        gate_bias = sb("gate_bias", [P, 2])
        row_cols = sb("row_cols", [P, 2, 3])
        held_cols = sb("held_cols", [P, 3])
        gate_z = sb("gate_z", [P, 2])
        denom = sb("denom", [P, 2, 4])
        inverse = sb("inverse", [P, 2, 4])
        row_w = sb("row_w", [P, 2])
        alpha = sb("alpha", [P, 2])
        stats = sb("stats", [P, 2, 6])
        factor = sb("factor", [P, 8])
        scratch = sb("scratch", [P, 16])
        norm = sb("norm", [P, 2, 2])

        z1 = [psum(f"z1_{n}", [P, D]) for n in range(2)]
        z2 = [psum(f"z2_{n}", [P, D]) for n in range(2)]
        zt = [psum(f"zt_{n}", [P, D]) for n in range(2)]
        proj = psum("proj", [P, D])
        misc = psum("misc", [P, D])
        l_psum = misc[:, 0:P]
        den_psum = misc[:, P:P + 1]

        staged = [sem(f"staged{n}") for n in range(STAGES)]
        vectors = sem("vectors")
        a_loaded = sem("a_loaded")
        bias_loaded = sem("bias_loaded")
        adj_loaded = [sem(f"adj_loaded{s}") for s in range(RING)]
        stored = [sem(f"stored{n}") for n in range(2)]
        ident_zero, ident_ready = sem("ident_zero"), sem("ident_ready")
        ones_ready = sem("ones_ready")
        v_dots, v_spread, v_ready = sem("v_dots"), sem("v_spread"), sem("v_ready")
        w_hi_ready, w_lo_ready = sem("w_hi_ready"), sem("w_lo_ready")
        x_hi_ready, r_dot, r_ready, x_lo_ready = sem("x_hi_ready"), sem("r_dot"), sem("r_ready"), sem("x_lo_ready")
        bias_neg = sem("bias_neg")
        cols_held = sem("cols_held")
        row_joined, row_dots, diag_ready = sem("row_joined"), sem("row_dots"), sem("diag_ready")
        l_spread, l_ready = sem("l_spread"), sem("l_ready")
        relu_done, exp_done, adj_r_ready = sem("relu_done"), sem("exp_done"), sem("adj_r_ready")
        masked, e_hi_ready, e_lo_ready, esum_ready = sem("masked"), sem("e_hi_ready"), sem("e_lo_ready"), sem("esum_ready")
        chunk_used, den_ready = sem("chunk_used"), sem("den_ready")
        z_dots, gate_exp = sem("z_dots"), sem("gate_exp")
        denoms, inverses, alpha_ready, zs_ready = sem("denoms"), sem("inverses"), sem("alpha_ready"), sem("zs_ready")
        zt_ready, zt_hi_ready, zt_lo_ready = sem("zt_ready"), sem("zt_hi_ready"), sem("zt_lo_ready")
        proj_ready, u_ready, tanh_ready = sem("proj_ready"), sem("u_ready"), sem("tanh_ready")
        y_steps, stats_ready = sem("y_steps"), sem("stats_ready")
        factor_ready, moment_steps, norm_ready, y_ready = (sem(n) for n in ("factor_ready", "moment_steps",
                                                                            "norm_ready", "y_ready"))

        block = ctx.enter_context(nc.Block())

        def since(eng, s, value):
            if not isinstance(value, int) or value > 0:
                eng.wait_ge(s, value)

        def for_tiles(eng, tile):
            tile(0, 0)
            tile(1, 1)
            with eng.Fori(1, TILES // 2 - 1) as pair:
                tile(pair * 2, 0)
                tile(pair * 2 + 1, 1)
            tile(LAST - 1, 0)
            tile(LAST, 1)

        def first(t):
            return isinstance(t, int) and t == 0

        def last(t):
            return isinstance(t, int) and t == LAST

        def has_older(t):
            return not isinstance(t, int) or t >= 2

        def x_rows(t):
            if isinstance(t, int):
                return x_hi[:, t, :].bitcast(F32), x_lo[:, t, :].bitcast(F32)
            return tuple(v[:, bass.ds(t, 1), :].rearrange("p o d -> p (o d)").bitcast(F32) for v in (x_hi, x_lo))

        @block.sync
        def _(sp):
            def load_stage(n):
                before = n - STAGES
                if 0 <= before < KT:
                    sp.wait_ge(v_dots, 2 * (before + 1))
                    sp.wait_ge(w_lo_ready, before + 1)
                elif before >= KT:
                    sp.wait_ge(x_lo_ready, before - KT + 1)
                if n < KT:
                    rows = w_sa[n]
                elif n < KT + TILES:
                    rows = x[n - KT]
                else:
                    rows = w_gcnb[n - KT - TILES]
                sp.dma_start(stage[n % STAGES], rows).then_inc(staged[n % STAGES], 16)

            def load_adj(t, c):
                j, n = CHUNKS[c]
                since(sp, masked, t * NC + (c - RING + 1))
                since(sp, adj_r_ready, t * NC + (c - RING + 1))
                sp.dma_start(adj[c % RING][:, :, :], adj_t[t, :, j:j + n, :]).then_inc(adj_loaded[c % RING], 16)

            def store(t, parity):
                sp.wait_ge(y_ready, t + 1)
                sp.dma_start(out[t], y[parity]).then_inc(stored[parity], 16)

            for n in range(KT):
                load_stage(n)
            for n in range(2):
                sp.dma_start(a_row[n], a_sa[:, n * D:(n + 1) * D].to_broadcast([P, D])).then_inc(a_loaded, 16)
            for n, w in enumerate((wa, wb)):
                sp.dma_start(w_gate[:, n, :, :].rearrange("p h d -> p (h d)"),
                             w.to_broadcast([P, 2 * D])).then_inc(vectors, 16)
            for n, b in enumerate((ba, bb)):
                sp.dma_start(gate_bias[:, n:n + 1], b.to_broadcast([P, 1])).then_inc(vectors, 16)

            def tile(t, parity):
                for c, (j, n) in enumerate(CHUNKS):
                    if first(t):
                        for jt in range(j, j + n):
                            load_stage(KT + jt)
                    load_adj(t, c)
                if first(t):
                    for k in range(KT):
                        load_stage(KT + TILES + k)
                    sp.wait_ge(x_lo_ready, TILES)
                    sp.dma_start(bias_row, b_gcnb.to_broadcast([P, D])).then_inc(bias_loaded, 16)
                if has_older(t):
                    store(t - 2, parity)

            for_tiles(sp, tile)
            store(LAST - 1, 0)
            store(LAST, 1)
            for n in range(2):
                sp.wait_ge(stored[n], 16 * TILES // 2)

        @block.gpsimd
        def _(pool):
            nc.gpsimd.memset(ident[:, :], 0.0).then_inc(ident_zero, 1)
            pool.wait_ge(ident_zero, 1)
            nc.gpsimd.affine_select(out=ident[:, :], in_=ident[:, :], compare_op=ALU.not_equal, fill=1.0, base=0,
                                    pattern=[[-1, P]], channel_multiplier=1).then_inc(ident_ready, 1)
            nc.gpsimd.memset(ones[:, :], 1.0).then_inc(ones_ready, 1)
            for n, value in enumerate((0.5, 1.0 / D, 0.25, EPS_NORM, -0.5, 1.5, 1.0)):
                nc.gpsimd.memset(factor[:, n:n + 1], value).then_inc(factor_ready, 1)
            pool.wait_ge(factor_ready, 7)

            def split_w(k, m):
                n = k if m == 0 else KT + TILES + k
                pool.wait_ge(staged[n % STAGES], 16 * (n // STAGES + 1))
                pool.wait_ge(w_hi_ready, m * KT + k + 1)
                nc.gpsimd.tensor_tensor(w_lo[:, m, k, :], stage[n % STAGES], w_hi[:, m, k, :].bitcast(F32),
                                        ALU.subtract).then_inc(w_lo_ready, 1)

            for m in range(2):
                for k in range(KT):
                    split_w(k, m)

            def moments(t, parity):
                s, m = stats[:, parity, :], scratch
                pool.wait_ge(stats_ready, t + 1)
                steps = [
                    (m[:, 0:2], s[:, 1:3], s[:, 4:6], ALU.add),
                    (m[:, 2:3], s[:, 1:2], s[:, 4:5], ALU.subtract),
                    (m[:, 3:4], m[:, 2:3], m[:, 2:3], ALU.mult),
                    (m[:, 4:6], m[:, 0:2], factor[:, 0:2], ALU.mult),
                    (m[:, 6:7], m[:, 3:4], factor[:, 2:3], ALU.mult),
                    (m[:, 7:8], m[:, 5:6], m[:, 6:7], ALU.add),
                    (m[:, 8:9], m[:, 7:8], factor[:, 3:4], ALU.add),
                    (m[:, 9:10], m[:, 8:9], factor[:, 4:5], ALU.pow),
                    (m[:, 10:11], m[:, 9:10], m[:, 9:10], ALU.mult),
                    (m[:, 11:12], m[:, 10:11], m[:, 8:9], ALU.mult),
                    (m[:, 12:13], m[:, 11:12], factor[:, 4:5], ALU.mult),
                    (m[:, 13:14], m[:, 12:13], factor[:, 5:6], ALU.add),
                    (norm[:, parity, 1:2], m[:, 13:14], m[:, 9:10], ALU.mult),
                    (norm[:, parity, 0:1], m[:, 4:5], factor[:, 6:7], ALU.mult),
                ]
                for n, (dst, a, b, op) in enumerate(steps):
                    if n:
                        pool.wait_ge(moment_steps, t * (len(steps) - 1) + n)
                    ins = nc.gpsimd.tensor_tensor(dst, a, b, op)
                    ins.then_inc(moment_steps if n < len(steps) - 1 else norm_ready, 1)

            for_tiles(pool, moments)

        @block.scalar
        def _(act):
            def w_part(k, m):
                n = k if m == 0 else KT + TILES + k
                act.wait_ge(staged[n % STAGES], 16 * (n // STAGES + 1))
                nc.scalar.copy(w_hi[:, m, k, :], stage[n % STAGES]).then_inc(w_hi_ready, 1)

            def x_part(jt):
                n = KT + jt
                act.wait_ge(staged[n % STAGES], 16 * (n // STAGES + 1))
                nc.scalar.copy(x_hi[:, jt, :], stage[n % STAGES]).then_inc(x_hi_ready, 1)

            def weights(t, parity, c):
                j, n = CHUNKS[c]
                e = e_raw[c % E_RING]
                if c == 0:
                    act.wait_ge(l_ready, t + 1)
                if first(t):
                    act.wait_ge(r_ready, 2 * (c + 1))
                since(act, esum_ready, t * NC + (c - E_RING + 1))
                for k in range(n):
                    ins = nc.scalar.activation(e[:, k, :], l_row[:, parity, :], ACT.Relu,
                                                bias=r_col[:, j + k:j + k + 1])
                ins.then_inc(relu_done, 1)
                act.wait_ge(relu_done, t * NC + (c + 1))
                for k in range(n):
                    ins = nc.scalar.activation(e[:, k, :], e[:, k, :], ACT.Exp, scale=SLOPE - 1.0,
                                                bias=r_neg[:, j + k:j + k + 1])
                ins.then_inc(exp_done, 1)

            def adjacency(t, c):
                act.wait_ge(adj_loaded[c % RING], (t * (NC // RING) + (c // RING + 1)) * 16)
                since(act, chunk_used, t * NC + (c - RING + 1))
                nc.scalar.copy(adj_r[c % RING][:, :, :], adj[c % RING][:, :, :]).then_inc(adj_r_ready, 1)

            def gate_exps(t, parity):
                act.wait_ge(z_dots, t * 2 + 2)
                act.wait_ge(cols_held, t + 1)
                for g in range(2):
                    nc.scalar.activation(denom[:, parity, g:g + 1], gate_z[:, g:g + 1], ACT.Exp, scale=-1.0,
                                         bias=held_cols[:, g:g + 1])
                nc.scalar.activation(row_w[:, parity:parity + 1], held_cols[:, 2:3], ACT.Exp,
                                     scale=-SLOPE).then_inc(gate_exp, 1)

            def zt_part(t):
                act.wait_ge(zt_ready, t + 1)
                since(act, proj_ready, t)
                for h in range(2):
                    ins = nc.scalar.copy(zt_hi[:, h, :], zt[h][:, :])
                ins.then_inc(zt_hi_ready, 1)

            def tanh_half(t, parity):
                act.wait_ge(u_ready, t + 1)
                nc.scalar.activation(y[parity], y[parity], ACT.Tanh, scale=0.5).then_inc(tanh_ready, 1)

            for k in range(KT):
                w_part(k, 0)

            def tile(t, parity):
                for c, (j, n) in enumerate(CHUNKS):
                    if first(t):
                        for jt in range(j, j + n):
                            x_part(jt)
                    weights(t, parity, c)
                    adjacency(t, c)
                    if c == 3 and not first(t):
                        gate_exps(t - 1, 1 - parity)
                        if has_older(t):
                            tanh_half(t - 2, parity)
                    if c == 5 and not first(t):
                        zt_part(t - 1)
                if first(t):
                    for k in range(KT):
                        w_part(k, 1)

            for_tiles(act, tile)
            gate_exps(LAST, 1)
            tanh_half(LAST - 1, 0)
            zt_part(LAST)
            tanh_half(LAST, 1)

        @block.tensor
        def _(pe):
            def spread_v():
                pe.wait_ge(ones_ready, 1)
                for h in range(2):
                    for k in range(KT):
                        pe.wait_ge(diag_ready, h * KT + k + 1)
                        nc.tensor.matmul(zt[h][:, k * P:(k + 1) * P], ones[:, :], diag[:, :], start=True,
                                         stop=True).then_inc(v_spread, 1)

            def spread_l(t):
                pe.wait_ge(diag_ready, t + (2 * KT + 1))
                nc.tensor.matmul(l_psum, ones[:, :], diag[:, :], start=True, stop=True).then_inc(l_spread, 1)

            def chunk(t, parity, c):
                j, n = CHUNKS[c]
                s = c % RING
                pe.wait_ge(adj_r_ready, t * NC + (c + 1))
                pe.wait_ge(e_lo_ready, t * NC + (c + 1))
                if first(t):
                    pe.wait_ge(x_lo_ready, j + n)
                if c == 0:
                    since(pe, zs_ready, t - 1)
                for k in range(n):
                    jt = j + k
                    begin, end = jt == 0, jt == TILES - 1
                    nc.tensor.matmul(z2[parity][:, :], adj_r[s][:, k, :], x_hi[:, jt, :], start=begin, stop=False)
                    nc.tensor.matmul(z2[parity][:, :], adj_r[s][:, k, :], x_lo[:, jt, :], start=False, stop=end)
                    nc.tensor.matmul(z1[parity][:, :], e_hi[s][:, k, :], x_hi[:, jt, :], start=begin, stop=False)
                    nc.tensor.matmul(z1[parity][:, :], e_hi[s][:, k, :], x_lo[:, jt, :], start=False, stop=False)
                    ins = nc.tensor.matmul(z1[parity][:, :], e_lo[s][:, k, :], x_hi[:, jt, :], start=False, stop=end)
                ins.then_inc(chunk_used, 1)

            def denominator(t, parity):
                pe.wait_ge(esum_ready, t * NC + NC)
                pe.wait_ge(l_ready, TILES if last(t) else t + 2)
                since(pe, denoms, t)
                for c in range(NC):
                    ins = nc.tensor.matmul(den_psum, esum[:, parity, c, :], ones[:, 0:1], start=(c == 0),
                                            stop=(c == NC - 1))
                ins.then_inc(den_ready, 1)

            def turn(t):
                pe.wait_ge(zs_ready, t + 1)
                since(pe, zt_lo_ready, t)
                for h in range(2):
                    for k in range(KT):
                        ins = nc.tensor.transpose(zt[h][:, k * P:(k + 1) * P], zs[:, h, k * P:(k + 1) * P],
                                                   ident[:, :])
                ins.then_inc(zt_ready, 1)

            def project(t):
                pe.wait_ge(zt_lo_ready, t + 1)
                if first(t):
                    pe.wait_ge(w_lo_ready, 2 * KT)
                since(pe, u_ready, t)
                steps = [(h, k, a, b) for h in range(2) for k in range(KT)
                         for a, b in ((zt_hi, w_hi), (zt_hi, w_lo), (zt_lo, w_hi))]
                for n, (h, k, a, b) in enumerate(steps):
                    ins = nc.tensor.matmul(proj[:, :], a[:, h, k * P:(k + 1) * P], b[:, h, k, :], start=(n == 0),
                                            stop=(n == len(steps) - 1))
                ins.then_inc(proj_ready, 1)

            spread_v()
            spread_l(0)

            def tile(t, parity):
                for c in range(NC):
                    chunk(t, parity, c)
                    if c == 0 and not last(t):
                        since(pe, denoms, t - 1)
                        spread_l(t + 1)
                    if c == 2 and not first(t):
                        turn(t - 1)
                    if c == 4 and not first(t):
                        project(t - 1)
                denominator(t, parity)

            for_tiles(pe, tile)
            turn(LAST)
            project(LAST)

        @block.vector
        def _(dve):
            def dot(in0, in1, scale, start, accum, done, count):
                since(dve, done, count)
                nc.vector.tensor_tensor_reduce(product[:, :], in0, in1, scale, start, ALU.mult, ALU.add,
                                               accum).then_inc(done, 1)

            dve.wait_ge(a_loaded, 32)
            for k in range(KT):
                dve.wait_ge(staged[k], 16)
                for h in range(2):
                    dot(stage[k], a_row[h], 1.0, 0.0, v_col[:, h, k:k + 1], v_dots, 2 * k + h)
            dve.wait_ge(ident_ready, 1)
            dve.wait_ge(v_dots, 2 * KT)
            for h in range(2):
                for k in range(KT):
                    since(dve, v_spread, h * KT + k)
                    nc.vector.tensor_scalar(diag[:, :], ident[:, :], v_col[:, h, k:k + 1], None, ALU.mult) \
                        .then_inc(diag_ready, 1)
            dve.wait_ge(v_spread, 2 * KT)
            nc.vector.tensor_copy(v_l[:, :], zt[0][:, :]).then_inc(v_ready, 1)
            nc.vector.tensor_copy(v_r, zt[1][:, :]).then_inc(v_ready, 1)
            dve.wait_ge(vectors, 16 * 4)
            nc.vector.tensor_scalar(gate_bias[:, :], gate_bias[:, :], -1.0, None, ALU.mult).then_inc(bias_neg, 1)
            dve.wait_ge(v_ready, 2)
            dve.wait_ge(bias_neg, 1)

            def sources(c):
                j, n = CHUNKS[c]
                for jt in range(j, j + n):
                    item = KT + jt
                    dve.wait_ge(staged[item % STAGES], 16 * (item // STAGES + 1))
                    dot(stage[item % STAGES], v_r, 1.0, 0.0, r_col[:, jt:jt + 1], r_dot, jt)
                    dve.wait_ge(x_hi_ready, jt + 1)
                    nc.vector.tensor_tensor(x_lo[:, jt, :], stage[item % STAGES], x_hi[:, jt, :].bitcast(F32),
                                            ALU.subtract).then_inc(x_lo_ready, 1)
                dve.wait_ge(r_dot, j + n)
                nc.vector.tensor_scalar(r_neg[:, j:j + n], r_col[:, j:j + n], -SLOPE, None, ALU.mult) \
                    .then_inc(r_ready, 2)

            def target(t, parity):
                hi, lo = x_rows(t)
                nc.vector.tensor_tensor(x_row[:, :], hi, lo, ALU.add).then_inc(row_joined, 1)
                dve.wait_ge(row_joined, t + 1)
                dot(x_row[:, :], v_l[:, :], 1.0, 0.0, row_cols[:, parity, 2:3], row_dots, t * 3)
                for g in range(2):
                    dot(x_row[:, :], w_gate[:, g, 1, :], -1.0, gate_bias[:, g:g + 1], row_cols[:, parity, g:g + 1],
                        row_dots, t * 3 + (g + 1))
                since(dve, l_spread, t)
                dve.wait_ge(row_dots, t * 3 + 3)
                nc.vector.tensor_scalar(diag[:, :], ident[:, :], row_cols[:, parity, 2:3], None, ALU.mult) \
                    .then_inc(diag_ready, 1)

            def hold_cols(t, parity):
                nc.vector.tensor_copy(held_cols[:, :], row_cols[:, parity, :]).then_inc(cols_held, 1)

            def l_copy(t, parity):
                dve.wait_ge(l_spread, t + 1)
                nc.vector.tensor_copy(l_row[:, parity, :], l_psum).then_inc(l_ready, 1)

            def parts(t, parity, c):
                n = CHUNKS[c][1]
                s = c % RING
                e = e_raw[c % E_RING][:, 0:n, :]
                count = t * NC + (c + 1)
                dve.wait_ge(exp_done, count)
                dve.wait_ge(adj_loaded[s], (t * (NC // RING) + (c // RING + 1)) * 16)
                nc.vector.scalar_tensor_tensor(e, adj[s][:, :, :], 0.0, e, ALU.not_equal, ALU.mult) \
                    .then_inc(masked, 1)
                dve.wait_ge(masked, count)
                since(dve, chunk_used, t * NC + (c - RING + 1))
                nc.vector.tensor_copy(e_hi[s][:, :, :], e).then_inc(e_hi_ready, 1)
                dve.wait_ge(e_hi_ready, count)
                nc.vector.tensor_tensor(e_lo[s][:, :, :], e, e_hi[s][:, :, :].bitcast(F32), ALU.subtract) \
                    .then_inc(e_lo_ready, 1)
                if c == 0:
                    since(dve, den_ready, t - 1)
                nc.vector.tensor_reduce(esum[:, parity, c, :], e.rearrange("p j i -> p i j"), AX_X, ALU.add) \
                    .then_inc(esum_ready, 1)

            def gate_dots(t, parity):
                dve.wait_ge(chunk_used, t * NC + NC)
                for g in range(2):
                    dot(z2[parity][:, :], w_gate[:, g, 0, :], 1.0, 0.0, gate_z[:, g:g + 1], z_dots, t * 2 + g)

            def scale_sums(t, parity):
                dve.wait_ge(gate_exp, t + 1)
                nc.vector.tensor_scalar(denom[:, parity, 0:2], denom[:, parity, 0:2], 1.0, None, ALU.add)
                dve.wait_ge(den_ready, t + 1)
                nc.vector.tensor_scalar(denom[:, parity, 2:3], den_psum, row_w[:, parity:parity + 1], EPS_ATTN,
                                        ALU.mult, ALU.add).then_inc(denoms, 1)
                dve.wait_ge(denoms, t + 1)
                nc.vector.reciprocal(inverse[:, parity, 0:3], denom[:, parity, 0:3]).then_inc(inverses, 1)
                dve.wait_ge(inverses, t + 1)
                nc.vector.scalar_tensor_tensor(alpha[:, parity:parity + 1], inverse[:, parity, 0:1],
                                               row_w[:, parity:parity + 1], inverse[:, parity, 2:3], ALU.mult,
                                               ALU.mult).then_inc(alpha_ready, 1)
                if first(t):
                    dve.wait_ge(w_lo_ready, 2 * KT)
                    dve.wait_ge(bias_loaded, 16)
                since(dve, zt_ready, t)
                nc.vector.tensor_scalar(zs[:, 1, :], z2[parity][:, :], inverse[:, parity, 1:2], None, ALU.mult)
                dve.wait_ge(alpha_ready, t + 1)
                nc.vector.tensor_scalar(zs[:, 0, :], z1[parity][:, :], alpha[:, parity:parity + 1], None, ALU.mult) \
                    .then_inc(zs_ready, 1)

            def zt_rest(t):
                dve.wait_ge(zt_hi_ready, t + 1)
                since(dve, proj_ready, t)
                for h in range(2):
                    ins = nc.vector.tensor_tensor(zt_lo[:, h, :], zt[h][:, :], zt_hi[:, h, :].bitcast(F32),
                                                   ALU.subtract)
                ins.then_inc(zt_lo_ready, 1)

            def add_bias(t, parity):
                dve.wait_ge(proj_ready, t + 1)
                if has_older(t):
                    dve.wait_ge(stored[parity], (t - parity) * 8)
                nc.vector.scalar_tensor_tensor(y[parity], bias_row, inverse[:, parity, 1:2], proj[:, :],
                                               ALU.mult, ALU.add).then_inc(u_ready, 1)

            def residual(t, parity):
                hi, lo = x_rows(t)
                dve.wait_ge(tanh_ready, t + 1)
                nc.vector.scalar_tensor_tensor(y[parity], y[parity], 0.5, lo, ALU.mult, ALU.add).then_inc(y_steps, 1)
                dve.wait_ge(y_steps, t * 2 + 1)
                nc.vector.scalar_tensor_tensor(y[parity], y[parity], 0.5, hi, ALU.add, ALU.add).then_inc(y_steps, 1)
                dve.wait_ge(y_steps, t * 2 + 2)
                nc.vector.bn_stats(stats[:, parity, :], y[parity]).then_inc(stats_ready, 1)

            def normalise(t, parity):
                dve.wait_ge(norm_ready, t + 1)
                nc.vector.tensor_scalar(y[parity], y[parity], norm[:, parity, 0:1], norm[:, parity, 1:2],
                                        ALU.subtract, ALU.mult).then_inc(y_ready, 1)

            def tile(t, parity):
                for c in range(NC):
                    if first(t):
                        sources(c)
                        if c == 0:
                            dve.wait_ge(x_lo_ready, CHUNKS[0][1])
                            target(0, 0)
                            l_copy(0, 0)
                    parts(t, parity, c)
                    if c == 0 and not first(t):
                        hold_cols(t - 1, 1 - parity)
                    if c == 0 and not last(t):
                        if not first(t):
                            dve.wait_ge(cols_held, t)
                        target(t + 1, 1 - parity)
                    if c == 2:
                        if has_older(t):
                            add_bias(t - 2, parity)
                        if not first(t):
                            gate_dots(t - 1, 1 - parity)
                    if c == 3:
                        if not last(t):
                            l_copy(t + 1, 1 - parity)
                        if not first(t):
                            scale_sums(t - 1, 1 - parity)
                    if c == 4 and has_older(t):
                        residual(t - 2, parity)
                    if c == 5:
                        if not first(t):
                            zt_rest(t - 1)
                        if has_older(t):
                            normalise(t - 2, parity)

            for_tiles(dve, tile)
            add_bias(LAST - 1, 0)
            hold_cols(LAST, 1)
            gate_dots(LAST, 1)
            scale_sums(LAST, 1)
            residual(LAST - 1, 0)
            zt_rest(LAST)
            normalise(LAST - 1, 0)
            add_bias(LAST, 1)
            residual(LAST, 1)
            normalise(LAST, 1)


def kernel(x, adj, L0_gnn_W_sa, L0_gnn_a_sa, L0_gnn_W_gcnb, L0_gnn_b_gcnb, L0_gnn_Wa, L0_gnn_ba, L0_gnn_Wb,
           L0_gnn_bb):
    import numpy as np
    import concourse.bacc as bacc
    from concourse.bass_utils import run_bass_kernel_spmd

    x = np.asarray(x)
    adj = np.asarray(adj)
    nodes, d = x.shape
    tiles = -(-nodes // P)
    x_pad = np.zeros((tiles * P, d), x.dtype)
    x_pad[:nodes] = x
    adj_pad = np.zeros((tiles * P, tiles * P), adj.dtype)
    adj_pad[:nodes, :nodes] = adj
    adj_t = adj_pad.reshape(tiles, P, tiles, P).transpose(0, 3, 2, 1)
    arrays = {
        "x": x_pad.reshape(tiles, P, d),
        "adj_t": adj_t,
        "w_sa": np.asarray(L0_gnn_W_sa).reshape(d // P, P, d),
        "a_sa": np.asarray(L0_gnn_a_sa),
        "w_gcnb": np.asarray(L0_gnn_W_gcnb).reshape(d // P, P, d),
        "b_gcnb": np.asarray(L0_gnn_b_gcnb).reshape(1, d),
        "wa": np.asarray(L0_gnn_Wa),
        "ba": np.asarray(L0_gnn_ba).reshape(1, 1),
        "wb": np.asarray(L0_gnn_Wb),
        "bb": np.asarray(L0_gnn_bb).reshape(1, 1),
    }
    arrays = {f"{name}_dram": np.ascontiguousarray(a) for name, a in arrays.items()}
    nc = bacc.Bacc("TRN2", target_bir_lowering=False, num_devices=1)
    args = [nc.dram_tensor(name, a.shape, mybir.dt.from_np(a.dtype), kind="ExternalInput").ap()
            for name, a in arrays.items()]
    out = nc.dram_tensor("out_dram", (tiles, P, d), F32, kind="ExternalOutput").ap()
    adj_resnorm_kernel(nc, *args, out)
    r = run_bass_kernel_spmd(nc, [arrays], core_ids=[0])
    return np.asarray(r.results[0]["out_dram"]).reshape(tiles * P, d)[:nodes]
```

```python
from contextlib import ExitStack

import concourse.bass as bass
from concourse import mybir

ALU = mybir.AluOpType
ACT = mybir.ActivationFunctionType
AX_X = mybir.AxisListType.X
F32 = mybir.dt.float32
F32R = mybir.dt.float32r
BF16 = mybir.dt.bfloat16

P = 128
SLOPE = 0.01
EPS_ATTN = 1e-5
EPS_NORM = 1e-5

RING = 3
E_RING = 2
STAGES = 8
AHEAD = 2


def chunks_of(tiles):
    sizes = [5, 4, 4, 5, 4, 4]
    assert sum(sizes) == tiles and len(sizes) % RING == 0 and len(sizes) % E_RING == 0
    return [(sum(sizes[:c]), n) for c, n in enumerate(sizes)]


def groups_of(tiles):
    sizes = [3] * 8 + [2]
    assert sum(sizes) == tiles and 2 * len(sizes) % RING == 0
    return [(sum(sizes[:g]), n) for g, n in enumerate(sizes)]


def adj_resnorm_kernel(nc, x, adj_t, w_sa, w_sa_t, a_sa, w_gcnb, b_gcnb, wa, ba, wb, bb, out):
    TILES, _, D = x.shape
    KT = D // P
    CHUNKS = chunks_of(TILES)
    NC = len(CHUNKS)
    GROUPS = groups_of(TILES)
    EARLY = 2 * len(GROUPS)
    LAST = TILES - 1
    group_of = [g for g, (_, n) in enumerate(GROUPS) for _ in range(n)]
    assert TILES % 2 == 0

    with ExitStack() as ctx:
        def sb(name, shape, dt=F32):
            return ctx.enter_context(nc.sbuf_tensor(name, shape, dt))

        def psum(name, shape):
            return ctx.enter_context(nc.psum_tensor(name, shape, F32))

        def sem(name):
            return ctx.enter_context(nc.semaphore(name))

        x_hi = sb("x_hi", [P, TILES, D], F32R)
        x_lo = sb("x_lo", [P, TILES, D], F32R)
        w_hi = sb("w_hi", [P, 2, KT, D], F32R)
        w_lo = sb("w_lo", [P, 2, KT, D], F32R)
        width = [CHUNKS[s][1] for s in range(RING)]
        adj = [sb(f"adj{s}", [P, width[s], P]) for s in range(RING)]
        adj_r = [sb(f"adj_r{s}", [P, width[s], P], F32R) for s in range(RING)]
        e_hi = [sb(f"e_hi{s}", [P, width[s], P], F32R) for s in range(RING)]
        e_lo = [sb(f"e_lo{s}", [P, width[s], P], F32R) for s in range(RING)]
        e_raw = [sb(f"e_raw{s}", [P, max(width), P]) for s in range(E_RING)]
        esums = sb("esums", [P, NC + 2, P])
        esum = esums[:, 0:NC, :]
        esum_all = esums[:, NC:NC + 2, :]
        zt_hi = sb("zt_hi", [P, 2, D], F32R)
        zt_lo = sb("zt_lo", [P, 2, D], F32R)
        work = sb("work", [P, 4, D])
        zs = work[:, 0:2, :]
        y = [work[:, 2, :], work[:, 3, :]]
        x_row = sb("x_row", [P, D])
        product = sb("product", [P, D], BF16)
        w_t = [e_raw[n][:, 0:KT, :].rearrange("p k i -> p (k i)") for n in range(E_RING)]
        w_t += [esums[:, n * KT:(n + 1) * KT, :].rearrange("p k i -> p (k i)") for n in range(2)]
        v_l = sb("v_l", [P, D])
        v_r = sb("v_r", [P, D])[:, :]
        work_a = [v[:, :].rearrange("p (k m) -> p k m", k=KT) for v in (v_l, x_row)]
        w_gate = sb("w_gate", [P, 2, 2, D])
        stage = [work[:, n, :] for n in range(4)] + [w_gate[:, n // 2, n % 2, :] for n in range(4)]
        bias_row = v_r
        ident = sb("ident", [P, P])
        ones = sb("ones", [P, P])
        diag = sb("diag", [P, P])
        l_row = sb("l_row", [P, 2, P])
        r_col = sb("r_col", [P, TILES])
        r_neg = sb("r_neg", [P, TILES])
        a_col = sb("a_col", [P, 2, KT])
        gate_bias = sb("gate_bias", [P, 2])
        row_cols = sb("row_cols", [P, 2, 3])
        held_cols = sb("held_cols", [P, 3])
        gate_z = sb("gate_z", [P, 2])
        denom = sb("denom", [P, 2, 4])
        gates = sb("gates", [P, 2, 2])
        inverse = sb("inverse", [P, 2])
        row_w = sb("row_w", [P, 2])
        alpha = sb("alpha", [P, 2])
        stats = sb("stats", [P, 2, 6])
        factor = sb("factor", [P, 8])
        scratch = sb("scratch", [P, 16])
        norm = sb("norm", [P, 2, 3])

        z1 = [psum(f"z1_{n}", [P, D]) for n in range(2)]
        z2 = [psum(f"z2_{n}", [P, D]) for n in range(2)]
        zt = [psum(f"zt_{n}", [P, D]) for n in range(2)]
        proj = psum("proj", [P, D])
        misc = psum("misc", [P, D])
        l_psum = misc[:, 0:P]
        den_psum = misc[:, P:P + 1]

        x_staged = [sem(f"x_staged{n}") for n in range(STAGES)]
        w_staged = [sem(f"w_staged{n}") for n in range(4)]
        vectors = sem("vectors")
        a_loaded = sem("a_loaded")
        w_t_loaded = [sem(f"w_t_loaded{k}") for k in range(KT)]
        bias_loaded = sem("bias_loaded")
        adj_loaded = [sem(f"adj_loaded{s}") for s in range(RING)]
        stored = [sem(f"stored{n}") for n in range(2)]
        ident_zero, ident_ready = sem("ident_zero"), sem("ident_ready")
        ones_ready = sem("ones_ready")
        a_spread, v_summed, v_ready = sem("a_spread"), sem("v_summed"), sem("v_ready")
        w_hi_ready, w_lo_ready = sem("w_hi_ready"), sem("w_lo_ready")
        x_hi_ready, r_dot, r_ready, x_lo_ready = sem("x_hi_ready"), sem("r_dot"), sem("r_ready"), sem("x_lo_ready")
        x_lo_first = sem("x_lo_first")
        bias_neg = sem("bias_neg")
        cols_held = sem("cols_held")
        row_joined, row_dots, diag_ready = sem("row_joined"), sem("row_dots"), sem("diag_ready")
        l_spread, l_ready = sem("l_spread"), sem("l_ready")
        relu_done, exp_done, adj_r_ready = sem("relu_done"), sem("exp_done"), sem("adj_r_ready")
        masked, e_hi_ready, e_lo_ready = sem("masked"), sem("e_hi_ready"), sem("e_lo_ready")
        esum_ready, esum_all_ready = sem("esum_ready"), sem("esum_all_ready")
        adj_r_used, parts_used, den_ready = sem("adj_r_used"), sem("parts_used"), sem("den_ready")
        z_dots, gate_exp = sem("z_dots"), sem("gate_exp")
        gate_denoms, gates_ready = sem("gate_denoms"), sem("gates_ready")
        denoms, inverses, alpha_ready, zs_ready = sem("denoms"), sem("inverses"), sem("alpha_ready"), sem("zs_ready")
        zt_ready, zt_hi_ready, zt_lo_ready = sem("zt_ready"), sem("zt_hi_ready"), sem("zt_lo_ready")
        proj_ready, u_ready, tanh_ready = sem("proj_ready"), sem("u_ready"), sem("tanh_ready")
        y_steps, stats_ready = sem("y_steps"), sem("stats_ready")
        factor_ready, moment_steps, norm_ready, y_ready = (sem(n) for n in ("factor_ready", "moment_steps",
                                                                            "norm_ready", "y_ready"))

        block = ctx.enter_context(nc.Block())

        def since(eng, s, value):
            if not isinstance(value, int) or value > 0:
                eng.wait_ge(s, value)

        def for_tiles(eng, tile, start=0):
            for t in range(start, 2):
                tile(t, t)
            with eng.Fori(1, TILES // 2 - 1) as pair:
                tile(pair * 2, 0)
                tile(pair * 2 + 1, 1)
            tile(LAST - 1, 0)

        def piece(t, c):
            return t * NC + (EARLY + c + (NC if last(t) else 0))

        def copied(t, c):
            return t * NC + (EARLY - 2 * NC + c)

        def adj_landed(eng, base, c):
            eng.wait_ge(adj_loaded[c % RING], base + (c // RING + 1) * 16)

        def loads_before(t, again=True):
            return t * (NC // RING * 16) + (EARLY // RING + (NC // RING if last(t) and again else 0)) * 16

        def first(t):
            return isinstance(t, int) and t == 0

        def last(t):
            return isinstance(t, int) and t == LAST

        def has_older(t):
            return not isinstance(t, int) or t >= 2

        def x_rows(t):
            if isinstance(t, int):
                return x_hi[:, t, :].bitcast(F32), x_lo[:, t, :].bitcast(F32)
            return tuple(v[:, bass.ds(t, 1), :].rearrange("p o d -> p (o d)").bitcast(F32) for v in (x_hi, x_lo))

        @block.sync
        def _(sp):
            def x_split(jt):
                g = group_of[jt]
                sp.wait_ge(r_dot, jt + 1)
                if jt == GROUPS[g][0]:
                    sp.wait_ge(x_lo_first, g + 1)
                else:
                    sp.wait_ge(x_lo_ready, jt - g)

            def load_x(g):
                for jt in range(GROUPS[g][0], sum(GROUPS[g])):
                    if jt >= STAGES:
                        x_split(jt - STAGES)
                    sp.dma_start(stage[jt % STAGES], x[jt]).then_inc(x_staged[jt % STAGES], 16)

            def load_w(n):
                if n < 4:
                    x_split(TILES - 1 - (TILES - 1 - n) % STAGES)
                else:
                    sp.wait_ge(w_lo_ready, n - 3)
                sp.dma_start(stage[n % 4], (w_sa, w_gcnb)[n // KT][n % KT]).then_inc(w_staged[n % 4], 16)

            def load_vectors():
                for n in range(4, STAGES):
                    x_split(TILES - 1 - (TILES - 1 - n) % STAGES)
                for g, w in enumerate((wa, wb)):
                    sp.dma_start(w_gate[:, g, :, :].rearrange("p h d -> p (h d)"),
                                 w.to_broadcast([P, 2 * D])).then_inc(vectors, 16)
                for g, b in enumerate((ba, bb)):
                    sp.dma_start(gate_bias[:, g:g + 1], b.to_broadcast([P, 1])).then_inc(vectors, 16)

            def load_early(number):
                g, t = number // 2, number % 2
                j, n = GROUPS[g]
                since(sp, adj_r_ready, number - RING + 1)
                sp.dma_start(adj[number % RING][:, 0:n, :], adj_t[t, :, j:j + n, :]) \
                    .then_inc(adj_loaded[number % RING], 16)

            def load_adj(t, c, copies, masks):
                j, n = CHUNKS[c]
                since(sp, adj_r_ready, copies)
                since(sp, masked, masks)
                sp.dma_start(adj[c % RING][:, :, :], adj_t[t, :, j:j + n, :]).then_inc(adj_loaded[c % RING], 16)

            def store(t, parity):
                sp.wait_ge(y_ready, t + 1)
                sp.dma_start(out[t], y[parity]).then_inc(stored[parity], 16)

            sp.dma_start(a_col[:, :, :], a_sa).then_inc(a_loaded, 16)
            for k in range(KT):
                sp.dma_start(w_t[k], w_sa_t[k]).then_inc(w_t_loaded[k], 16)
            load_x(0)
            for number in range(RING):
                load_early(number)
            for g in range(1, AHEAD + 1):
                load_x(g)
            for g in range(1, len(GROUPS)):
                for number in (2 * g + 1, 2 * g + 2):
                    if number < EARLY:
                        load_early(number)
                if g + AHEAD < len(GROUPS):
                    load_x(g + AHEAD)
                if g + AHEAD == len(GROUPS) - 1:
                    load_vectors()

            def tile(t, parity):
                for c in range(NC):
                    if isinstance(t, int) and t < 2:
                        load_adj(t, c, EARLY - RING + c + 1 if t * NC + c < RING else 0, t * NC + (c - RING + 1))
                    else:
                        load_adj(t, c, 0, t * NC + (c - RING + 1))
                    if first(t) and c >= 2:
                        for n in range(4) if c == 2 else (c + 1,):
                            load_w(n)
                if first(t):
                    load_w(7)
                    sp.wait_ge(r_dot, TILES)
                    sp.dma_start(bias_row, b_gcnb.to_broadcast([P, D])).then_inc(bias_loaded, 16)
                if has_older(t):
                    store(t - 2, parity)

            for_tiles(sp, tile)
            for c in range(NC):
                load_adj(LAST, c, copied(LAST, c) - (RING - 1), LAST * NC + min(c - RING + 1, 0))
            for c in range(NC):
                load_adj(LAST, c, copied(LAST, NC), LAST * NC + (c - RING + 1))
            store(LAST - 2, 1)
            store(LAST - 1, 0)
            store(LAST, 1)
            for n in range(2):
                sp.wait_ge(stored[n], 16 * TILES // 2)

        @block.gpsimd
        def _(pool):
            nc.gpsimd.memset(ident[:, :], 0.0).then_inc(ident_zero, 1)
            pool.wait_ge(ident_zero, 1)
            nc.gpsimd.affine_select(out=ident[:, :], in_=ident[:, :], compare_op=ALU.not_equal, fill=1.0, base=0,
                                    pattern=[[-1, P]], channel_multiplier=1).then_inc(ident_ready, 1)
            nc.gpsimd.memset(ones[:, :], 1.0).then_inc(ones_ready, 1)
            for n, value in enumerate((0.5, 1.0 / D, 0.25, EPS_NORM, -0.5, 1.5)):
                nc.gpsimd.memset(factor[:, n:n + 1], value).then_inc(factor_ready, 1)
            pool.wait_ge(factor_ready, 6)

            for g, (jt, _) in enumerate(GROUPS):
                pool.wait_ge(x_hi_ready, jt + 1)
                pool.wait_ge(x_staged[jt % STAGES], 16 * (jt // STAGES + 1))
                nc.gpsimd.tensor_tensor(x_lo[:, jt, :], stage[jt % STAGES], x_hi[:, jt, :].bitcast(F32),
                                        ALU.subtract).then_inc(x_lo_first, 1)

            for n in range(2 * KT):
                m, k = n // KT, n % KT
                pool.wait_ge(w_hi_ready, n + 1)
                pool.wait_ge(w_staged[n % 4], 16 * (n // 4 + 1))
                nc.gpsimd.tensor_tensor(w_lo[:, m, k, :], stage[n % 4], w_hi[:, m, k, :].bitcast(F32),
                                        ALU.subtract).then_inc(w_lo_ready, 1)

            def moments(t, parity):
                s, m = stats[:, parity, :], scratch
                pool.wait_ge(stats_ready, t + 1)
                steps = [
                    (m[:, 0:2], s[:, 1:3], s[:, 4:6], ALU.add),
                    (m[:, 2:3], s[:, 1:2], s[:, 4:5], ALU.subtract),
                    (m[:, 3:4], m[:, 2:3], m[:, 2:3], ALU.mult),
                    (norm[:, parity, 0:2], m[:, 0:2], factor[:, 0:2], ALU.mult),
                    (m[:, 6:7], m[:, 3:4], factor[:, 2:3], ALU.mult),
                    (m[:, 7:8], norm[:, parity, 1:2], m[:, 6:7], ALU.add),
                    (m[:, 8:9], m[:, 7:8], factor[:, 3:4], ALU.add),
                    (m[:, 9:10], m[:, 8:9], factor[:, 4:5], ALU.pow),
                    (m[:, 10:11], m[:, 9:10], m[:, 9:10], ALU.mult),
                    (m[:, 11:12], m[:, 10:11], m[:, 8:9], ALU.mult),
                    (m[:, 12:13], m[:, 11:12], factor[:, 4:5], ALU.mult),
                    (m[:, 13:14], m[:, 12:13], factor[:, 5:6], ALU.add),
                    (norm[:, parity, 2:3], m[:, 13:14], m[:, 9:10], ALU.mult),
                ]
                for n, (dst, a, b, op) in enumerate(steps):
                    if n:
                        pool.wait_ge(moment_steps, t * (len(steps) - 1) + n)
                    ins = nc.gpsimd.tensor_tensor(dst, a, b, op)
                    ins.then_inc(moment_steps if n < len(steps) - 1 else norm_ready, 1)

            for_tiles(pool, moments)
            moments(LAST, 1)

        @block.scalar
        def _(act):
            def w_part(n):
                act.wait_ge(w_staged[n % 4], 16 * (n // 4 + 1))
                nc.scalar.copy(w_hi[:, n // KT, n % KT, :], stage[n % 4]).then_inc(w_hi_ready, 1)

            def x_part(jt):
                act.wait_ge(x_staged[jt % STAGES], 16 * (jt // STAGES + 1))
                nc.scalar.copy(x_hi[:, jt, :], stage[jt % STAGES]).then_inc(x_hi_ready, 1)

            def weights(t, parity, c):
                j, n = CHUNKS[c]
                e = e_raw[c % E_RING]
                if c == 0:
                    act.wait_ge(l_ready, t + 1)
                if first(t):
                    act.wait_ge(r_ready, j + n)
                since(act, esum_ready, t * NC + (c - E_RING + 1))
                for k in range(n):
                    ins = nc.scalar.activation(e[:, k, :], l_row[:, parity, :], ACT.Relu,
                                                bias=r_col[:, j + k:j + k + 1])
                ins.then_inc(relu_done, 1)
                act.wait_ge(relu_done, t * NC + (c + 1))
                for k in range(n):
                    ins = nc.scalar.activation(e[:, k, :], e[:, k, :], ACT.Exp, scale=SLOPE - 1.0,
                                                bias=r_neg[:, j + k:j + k + 1])
                ins.then_inc(exp_done, 1)

            def adjacency(t, c):
                adj_landed(act, loads_before(t, again=False), c)
                act.wait_ge(adj_r_used, copied(t, c) - (RING - 1))
                nc.scalar.copy(adj_r[c % RING][:, :, :], adj[c % RING][:, :, :]).then_inc(adj_r_ready, 1)

            def adjacency_early(number):
                n = GROUPS[number // 2][1]
                act.wait_ge(adj_loaded[number % RING], (number // RING + 1) * 16)
                since(act, adj_r_used, number - RING + 1)
                nc.scalar.copy(adj_r[number % RING][:, 0:n, :], adj[number % RING][:, 0:n, :]) \
                    .then_inc(adj_r_ready, 1)

            def gate_exps(t, parity):
                act.wait_ge(z_dots, t * 2 + 2)
                act.wait_ge(cols_held, t + 1)
                for g in range(2):
                    nc.scalar.activation(denom[:, parity, g:g + 1], gate_z[:, g:g + 1], ACT.Exp, scale=-1.0,
                                         bias=held_cols[:, g:g + 1])
                nc.scalar.activation(row_w[:, parity:parity + 1], held_cols[:, 2:3], ACT.Exp,
                                     scale=-SLOPE).then_inc(gate_exp, 1)

            def zt_part(t, h):
                act.wait_ge(zt_ready, t * 2 + (2 - h))
                since(act, proj_ready, t * 2 - h)
                nc.scalar.copy(zt_hi[:, h, :], zt[h][:, :]).then_inc(zt_hi_ready, 1)

            def tanh_half(t, parity):
                act.wait_ge(u_ready, t + 1)
                nc.scalar.activation(y[parity], y[parity], ACT.Tanh, scale=0.5).then_inc(tanh_ready, 1)

            for jt in range(GROUPS[0][1]):
                x_part(jt)
            act.wait_ge(v_summed, KT)
            nc.scalar.copy(v_r, zt[1][:, :]).then_inc(v_ready, 1)
            for g in range(len(GROUPS)):
                if g == 0:
                    adjacency_early(0)
                    adjacency_early(1)
                if g + 1 < len(GROUPS):
                    for jt in range(GROUPS[g + 1][0], sum(GROUPS[g + 1])):
                        x_part(jt)
                if g > 0:
                    adjacency_early(2 * g)
                    adjacency_early(2 * g + 1)
                if g == 1:
                    act.wait_ge(v_summed, 2 * KT)
                    nc.scalar.copy(v_l[:, :], zt[0][:, :]).then_inc(v_ready, 1)
                if g in (5, 6):
                    weights(0, 0, g - 5)

            def tile(t, parity):
                for c in range(NC):
                    if not (first(t) and c < 2):
                        weights(t, parity, c)
                    if has_older(t):
                        adjacency(t, c)
                    if not has_older(t) and 2 <= t * NC + c < 2 * KT + 2:
                        w_part(t * NC + c - 2)
                    if c == 3 and not first(t):
                        gate_exps(t - 1, 1 - parity)
                        if has_older(t):
                            tanh_half(t - 2, parity)
                    if c == 5 and not first(t):
                        zt_part(t - 1, 1)
                        zt_part(t - 1, 0)

            for_tiles(act, tile)
            for c in range(NC):
                adjacency(LAST, c)
                if c < 2:
                    weights(LAST, 1, c)
                if c == 2:
                    gate_exps(LAST - 1, 0)
                    tanh_half(LAST - 2, 1)
            zt_part(LAST - 1, 1)
            zt_part(LAST - 1, 0)
            weights(LAST, 1, 2)
            weights(LAST, 1, 3)
            gate_exps(LAST, 1)
            weights(LAST, 1, 4)
            weights(LAST, 1, 5)
            zt_part(LAST, 1)
            tanh_half(LAST - 1, 0)
            zt_part(LAST, 0)
            tanh_half(LAST, 1)

        @block.tensor
        def _(pe):
            def sum_v():
                for h in (1, 0):
                    for k in range(KT):
                        pe.wait_ge(a_spread, (1 - h) * KT + k + 1)
                        pe.wait_ge(w_t_loaded[k], 16)
                        nc.tensor.matmul(zt[h][:, :], work_a[h][:, k, :], w_t[k], start=(k == 0),
                                         stop=(k == KT - 1)).then_inc(v_summed, 1)

            def spread_l(t):
                pe.wait_ge(diag_ready, t + 1)
                nc.tensor.matmul(l_psum, ones[:, :], diag[:, :], start=True, stop=True).then_inc(l_spread, 1)

            def sum_z2(buffer, parity, j, n):
                for k in range(n):
                    jt = j + k
                    nc.tensor.matmul(z2[parity][:, :], buffer[:, k, :], x_hi[:, jt, :], start=(jt == 0), stop=False)
                    ins = nc.tensor.matmul(z2[parity][:, :], buffer[:, k, :], x_lo[:, jt, :], start=False,
                                           stop=(jt == TILES - 1))
                ins.then_inc(adj_r_used, 1)

            def early(g, t):
                j, n = GROUPS[g]
                number = 2 * g + t
                pe.wait_ge(adj_r_ready, number + 1)
                pe.wait_ge(x_lo_ready, j + n - (g + 1))
                pe.wait_ge(x_lo_first, g + 1)
                sum_z2(adj_r[number % RING], t, j, n)

            def chunk_z2(t, parity, c):
                pe.wait_ge(adj_r_ready, copied(t, c) + 1)
                if c == 0:
                    pe.wait_ge(zs_ready, t * 2 - 2)
                sum_z2(adj_r[c % RING], parity, *CHUNKS[c])

            def chunk_z1(t, parity, c):
                j, n = CHUNKS[c]
                s = c % RING
                pe.wait_ge(e_lo_ready, t * NC + (c + 1))
                for k in range(n):
                    jt = j + k
                    nc.tensor.matmul(z1[parity][:, :], e_hi[s][:, k, :], x_hi[:, jt, :], start=(jt == 0), stop=False)
                    nc.tensor.matmul(z1[parity][:, :], e_hi[s][:, k, :], x_lo[:, jt, :], start=False, stop=False)
                    ins = nc.tensor.matmul(z1[parity][:, :], e_lo[s][:, k, :], x_hi[:, jt, :], start=False,
                                           stop=(jt == TILES - 1))
                ins.then_inc(parts_used, 1)

            def denominator(t, parity):
                pe.wait_ge(esum_all_ready, t + 1)
                if last(t):
                    pe.wait_ge(esum_ready, LAST * NC + NC)
                pe.wait_ge(l_ready, TILES if last(t) else t + 2)
                since(pe, denoms, t)
                ins = nc.tensor.matmul(den_psum, esum_all[:, parity, :], ones[:, 0:1], start=True, stop=not last(t))
                if last(t):
                    ins = nc.tensor.matmul(den_psum, esum[:, NC - 1, :], ones[:, 0:1], start=False, stop=True)
                ins.then_inc(den_ready, 1)

            def turn(t, h):
                pe.wait_ge(zs_ready, t * 2 + (2 - h))
                since(pe, zt_lo_ready, t * 2 - h)
                for k in range(KT):
                    ins = nc.tensor.transpose(zt[h][:, k * P:(k + 1) * P], zs[:, h, k * P:(k + 1) * P], ident[:, :])
                ins.then_inc(zt_ready, 1)

            def project(t, h):
                pe.wait_ge(zt_lo_ready, t * 2 + (2 - h))
                if h == 1:
                    if first(t):
                        pe.wait_ge(w_lo_ready, 2 * KT)
                    since(pe, u_ready, t)
                for k in range(KT):
                    for a, b in ((zt_hi, w_hi), (zt_hi, w_lo), (zt_lo, w_hi)):
                        ins = nc.tensor.matmul(proj[:, :], a[:, h, k * P:(k + 1) * P], b[:, h, k, :],
                                               start=(h == 1 and k == 0 and a is zt_hi and b is w_hi),
                                               stop=(h == 0 and k == KT - 1 and a is zt_lo))
                ins.then_inc(proj_ready, 1)

            sum_v()
            for g in range(len(GROUPS)):
                for t in range(2):
                    early(g, t)
                if g == 2:
                    spread_l(0)

            def tile(t, parity):
                for c in range(NC):
                    if has_older(t):
                        chunk_z2(t, parity, c)
                    chunk_z1(t, parity, c)
                    if c == 0:
                        since(pe, denoms, t - 1)
                        spread_l(t + 1)
                    if c == 2 and not first(t):
                        turn(t - 1, 1)
                        turn(t - 1, 0)
                    if c == 4 and not first(t):
                        project(t - 1, 1)
                        project(t - 1, 0)
                denominator(t, parity)

            for_tiles(pe, tile)
            for c in range(NC):
                chunk_z2(LAST, 1, c)
                if c == 2:
                    turn(LAST - 1, 1)
                    turn(LAST - 1, 0)
            chunk_z1(LAST, 1, 0)
            project(LAST - 1, 1)
            project(LAST - 1, 0)
            for c in range(1, NC):
                chunk_z1(LAST, 1, c)
                if c == 4:
                    turn(LAST, 1)
            denominator(LAST, 1)
            project(LAST, 1)
            turn(LAST, 0)
            project(LAST, 0)

        @block.vector
        def _(dve):
            def dot(in0, in1, scale, start, accum, done, count):
                since(dve, done, count)
                nc.vector.tensor_tensor_reduce(product[:, :], in0, in1, scale, start, ALU.mult, ALU.add,
                                               accum).then_inc(done, 1)

            dve.wait_ge(a_loaded, 16)
            dve.wait_ge(ones_ready, 1)
            for h in (1, 0):
                for k in range(KT):
                    nc.vector.tensor_scalar(work_a[h][:, k, :], ones[:, :], a_col[:, h, k:k + 1], None, ALU.mult) \
                        .then_inc(a_spread, 1)
            def sources(g):
                j, n = GROUPS[g]
                for jt in range(j, j + n):
                    dve.wait_ge(x_staged[jt % STAGES], 16 * (jt // STAGES + 1))
                    dot(stage[jt % STAGES], v_r, 1.0, 0.0, r_col[:, jt:jt + 1], r_dot, jt)
                    if jt > j:
                        dve.wait_ge(x_hi_ready, jt + 1)
                        nc.vector.tensor_tensor(x_lo[:, jt, :], stage[jt % STAGES], x_hi[:, jt, :].bitcast(F32),
                                                ALU.subtract).then_inc(x_lo_ready, 1)
                dve.wait_ge(r_dot, j + n)
                nc.vector.tensor_scalar(r_neg[:, j:j + n], r_col[:, j:j + n], -SLOPE, None, ALU.mult) \
                    .then_inc(r_ready, n)

            def target_l(t, parity):
                hi, lo = x_rows(t)
                since(dve, row_dots, t * 3)
                nc.vector.tensor_tensor(x_row[:, :], hi, lo, ALU.add).then_inc(row_joined, 1)
                dve.wait_ge(row_joined, t + 1)
                dot(x_row[:, :], v_l[:, :], 1.0, 0.0, row_cols[:, parity, 2:3], row_dots, t * 3)
                since(dve, l_spread, t)
                dve.wait_ge(row_dots, t * 3 + 1)
                nc.vector.tensor_scalar(diag[:, :], ident[:, :], row_cols[:, parity, 2:3], None, ALU.mult) \
                    .then_inc(diag_ready, 1)

            def target_gates(t, parity):
                for g in range(2):
                    dot(x_row[:, :], w_gate[:, g, 1, :], -1.0, gate_bias[:, g:g + 1], row_cols[:, parity, g:g + 1],
                        row_dots, t * 3 + (g + 1))

            def hold_cols(t, parity):
                nc.vector.tensor_copy(held_cols[:, :], row_cols[:, parity, :]).then_inc(cols_held, 1)

            def l_copy(t, parity):
                dve.wait_ge(l_spread, t + 1)
                nc.vector.tensor_copy(l_row[:, parity, :], l_psum).then_inc(l_ready, 1)

            def parts(t, parity, c):
                n = CHUNKS[c][1]
                s = c % RING
                e = e_raw[c % E_RING][:, 0:n, :]
                count = t * NC + (c + 1)
                dve.wait_ge(exp_done, count)
                adj_landed(dve, loads_before(t), c)
                if has_older(t) and not last(t):
                    dve.wait_ge(adj_r_ready, copied(t, c) + 1)
                nc.vector.scalar_tensor_tensor(e, adj[s][:, :, :], 0.0, e, ALU.not_equal, ALU.mult) \
                    .then_inc(masked, 1)
                dve.wait_ge(masked, count)
                since(dve, parts_used, t * NC + (c - RING + 1))
                nc.vector.tensor_copy(e_hi[s][:, :, :], e).then_inc(e_hi_ready, 1)
                dve.wait_ge(e_hi_ready, count)
                nc.vector.tensor_tensor(e_lo[s][:, :, :], e, e_hi[s][:, :, :].bitcast(F32), ALU.subtract) \
                    .then_inc(e_lo_ready, 1)
                nc.vector.tensor_reduce(esum[:, c, :], e.rearrange("p j i -> p i j"), AX_X, ALU.add) \
                    .then_inc(esum_ready, 1)

            def join_esum(t, parity):
                n = NC - 1 if last(t) else NC
                dve.wait_ge(esum_ready, t * NC + n)
                since(dve, den_ready, t - 1)
                nc.vector.tensor_reduce(esum_all[:, parity, :], esum[:, 0:n, :].rearrange("p c i -> p i c"), AX_X,
                                        ALU.add).then_inc(esum_all_ready, 1)

            def gate_dots(t, parity):
                if last(t):
                    dve.wait_ge(adj_r_used, copied(LAST, NC))
                else:
                    dve.wait_ge(parts_used, t * NC + NC)
                for g in range(2):
                    dot(z2[parity][:, :], w_gate[:, g, 0, :], 1.0, 0.0, gate_z[:, g:g + 1], z_dots, t * 2 + g)

            def scale_z2(t, parity):
                dve.wait_ge(gate_exp, t + 1)
                nc.vector.tensor_scalar(denom[:, parity, 0:2], denom[:, parity, 0:2], 1.0, None, ALU.add) \
                    .then_inc(gate_denoms, 1)
                dve.wait_ge(gate_denoms, t + 1)
                nc.vector.reciprocal(gates[:, parity, :], denom[:, parity, 0:2]).then_inc(gates_ready, 1)
                dve.wait_ge(gates_ready, t + 1)
                if first(t):
                    dve.wait_ge(w_lo_ready, 2 * KT)
                    dve.wait_ge(bias_loaded, 16)
                since(dve, zt_ready, t * 2)
                nc.vector.tensor_scalar(zs[:, 1, :], z2[parity][:, :], gates[:, parity, 1:2], None, ALU.mult) \
                    .then_inc(zs_ready, 1)

            def scale_z1(t, parity):
                dve.wait_ge(den_ready, t + 1)
                nc.vector.tensor_scalar(denom[:, parity, 2:3], den_psum, row_w[:, parity:parity + 1], EPS_ATTN,
                                        ALU.mult, ALU.add).then_inc(denoms, 1)
                dve.wait_ge(denoms, t + 1)
                nc.vector.reciprocal(inverse[:, parity:parity + 1], denom[:, parity, 2:3]).then_inc(inverses, 1)
                dve.wait_ge(inverses, t + 1)
                nc.vector.scalar_tensor_tensor(alpha[:, parity:parity + 1], gates[:, parity, 0:1],
                                               row_w[:, parity:parity + 1], inverse[:, parity:parity + 1], ALU.mult,
                                               ALU.mult).then_inc(alpha_ready, 1)
                dve.wait_ge(alpha_ready, t + 1)
                nc.vector.tensor_scalar(zs[:, 0, :], z1[parity][:, :], alpha[:, parity:parity + 1], None, ALU.mult) \
                    .then_inc(zs_ready, 1)

            def zt_rest(t, h):
                dve.wait_ge(zt_hi_ready, t * 2 + (2 - h))
                since(dve, proj_ready, t * 2 - h)
                nc.vector.tensor_tensor(zt_lo[:, h, :], zt[h][:, :], zt_hi[:, h, :].bitcast(F32),
                                        ALU.subtract).then_inc(zt_lo_ready, 1)

            def add_bias(t, parity):
                dve.wait_ge(proj_ready, t * 2 + 2)
                if has_older(t):
                    dve.wait_ge(stored[parity], (t - parity) * 8)
                nc.vector.scalar_tensor_tensor(y[parity], bias_row, gates[:, parity, 1:2], proj[:, :],
                                               ALU.mult, ALU.add).then_inc(u_ready, 1)

            def residual(t, parity):
                hi, lo = x_rows(t)
                dve.wait_ge(tanh_ready, t + 1)
                nc.vector.scalar_tensor_tensor(y[parity], y[parity], 0.5, lo, ALU.mult, ALU.add).then_inc(y_steps, 1)
                dve.wait_ge(y_steps, t * 2 + 1)
                nc.vector.scalar_tensor_tensor(y[parity], y[parity], 0.5, hi, ALU.add, ALU.add).then_inc(y_steps, 1)
                dve.wait_ge(y_steps, t * 2 + 2)
                nc.vector.bn_stats(stats[:, parity, :], y[parity]).then_inc(stats_ready, 1)

            def normalise(t, parity):
                dve.wait_ge(norm_ready, t + 1)
                nc.vector.tensor_scalar(y[parity], y[parity], norm[:, parity, 0:1], norm[:, parity, 2:3],
                                        ALU.subtract, ALU.mult).then_inc(y_ready, 1)

            dve.wait_ge(v_ready, 1)
            for g in range(len(GROUPS)):
                sources(g)
                if g == 2:
                    dve.wait_ge(v_ready, 2)
                    dve.wait_ge(x_lo_first, 1)
                    target_l(0, 0)
                if g == 4:
                    l_copy(0, 0)

            def tile(t, parity):
                for c in range(NC):
                    parts(t, parity, c)
                    if c == 0:
                        if first(t):
                            dve.wait_ge(vectors, 16 * 4)
                            nc.vector.tensor_scalar(gate_bias[:, :], gate_bias[:, :], -1.0, None, ALU.mult) \
                                .then_inc(bias_neg, 1)
                            dve.wait_ge(bias_neg, 1)
                            target_gates(0, 0)
                        else:
                            hold_cols(t - 1, 1 - parity)
                            dve.wait_ge(cols_held, t)
                        target_l(t + 1, 1 - parity)
                        target_gates(t + 1, 1 - parity)
                    if c == 2:
                        if has_older(t):
                            add_bias(t - 2, parity)
                        if not first(t):
                            gate_dots(t - 1, 1 - parity)
                    if c == 3:
                        l_copy(t + 1, 1 - parity)
                        if not first(t):
                            scale_z2(t - 1, 1 - parity)
                            scale_z1(t - 1, 1 - parity)
                    if c == 4 and has_older(t):
                        residual(t - 2, parity)
                    if c == 5:
                        join_esum(t, parity)
                        if not first(t):
                            zt_rest(t - 1, 1)
                            zt_rest(t - 1, 0)
                        if has_older(t):
                            normalise(t - 2, parity)

            dve.wait_ge(x_lo_first, len(GROUPS))
            for_tiles(dve, tile)
            add_bias(LAST - 2, 1)
            hold_cols(LAST - 1, 0)
            gate_dots(LAST - 1, 0)
            scale_z2(LAST - 1, 0)
            scale_z1(LAST - 1, 0)
            dve.wait_ge(gate_exp, LAST)
            hold_cols(LAST, 1)
            residual(LAST - 2, 1)
            zt_rest(LAST - 1, 1)
            zt_rest(LAST - 1, 0)
            for c in range(3):
                parts(LAST, 1, c)
            normalise(LAST - 2, 1)
            parts(LAST, 1, 3)
            gate_dots(LAST, 1)
            parts(LAST, 1, 4)
            scale_z2(LAST, 1)
            join_esum(LAST, 1)
            parts(LAST, 1, 5)
            add_bias(LAST - 1, 0)
            zt_rest(LAST, 1)
            scale_z1(LAST, 1)
            zt_rest(LAST, 0)
            residual(LAST - 1, 0)
            normalise(LAST - 1, 0)
            add_bias(LAST, 1)
            residual(LAST, 1)
            normalise(LAST, 1)


def kernel(x, adj, L0_gnn_W_sa, L0_gnn_a_sa, L0_gnn_W_gcnb, L0_gnn_b_gcnb, L0_gnn_Wa, L0_gnn_ba, L0_gnn_Wb,
           L0_gnn_bb):
    import numpy as np
    import concourse.bacc as bacc
    from concourse.bass_utils import run_bass_kernel_spmd

    x = np.asarray(x)
    adj = np.asarray(adj)
    nodes, d = x.shape
    tiles = -(-nodes // P)
    x_pad = np.zeros((tiles * P, d), x.dtype)
    x_pad[:nodes] = x
    adj_pad = np.zeros((tiles * P, tiles * P), adj.dtype)
    adj_pad[:nodes, :nodes] = adj
    adj_t = adj_pad.reshape(tiles, P, tiles, P).transpose(0, 3, 2, 1)
    arrays = {
        "x": x_pad.reshape(tiles, P, d),
        "adj_t": adj_t,
        "w_sa": np.asarray(L0_gnn_W_sa).reshape(d // P, P, d),
        "w_sa_t": np.asarray(L0_gnn_W_sa).T.reshape(d // P, P, d),
        "a_sa": np.asarray(L0_gnn_a_sa).reshape(2, d // P, P).transpose(2, 0, 1),
        "w_gcnb": np.asarray(L0_gnn_W_gcnb).reshape(d // P, P, d),
        "b_gcnb": np.asarray(L0_gnn_b_gcnb).reshape(1, d),
        "wa": np.asarray(L0_gnn_Wa),
        "ba": np.asarray(L0_gnn_ba).reshape(1, 1),
        "wb": np.asarray(L0_gnn_Wb),
        "bb": np.asarray(L0_gnn_bb).reshape(1, 1),
    }
    arrays = {f"{name}_dram": np.ascontiguousarray(a) for name, a in arrays.items()}
    nc = bacc.Bacc("TRN2", target_bir_lowering=False, num_devices=1)
    args = [nc.dram_tensor(name, a.shape, mybir.dt.from_np(a.dtype), kind="ExternalInput").ap()
            for name, a in arrays.items()]
    out = nc.dram_tensor("out_dram", (tiles, P, d), F32, kind="ExternalOutput").ap()
    adj_resnorm_kernel(nc, *args, out)
    r = run_bass_kernel_spmd(nc, [arrays], core_ids=[0])
    return np.asarray(r.results[0]["out_dram"]).reshape(tiles * P, d)[:nodes]
```

```python
from contextlib import ExitStack

import concourse.bass as bass
from concourse import mybir

ALU = mybir.AluOpType
ACT = mybir.ActivationFunctionType
AX_X = mybir.AxisListType.X
F32 = mybir.dt.float32
F32R = mybir.dt.float32r
BF16 = mybir.dt.bfloat16

P = 128
SLOPE = 0.01
EPS_ATTN = 1e-5
EPS_NORM = 1e-5

RING = 3
E_RING = 2
STAGES = 8
AHEAD = 2


def chunks_of(tiles):
    sizes = [5, 4, 4, 5, 4, 4]
    assert sum(sizes) == tiles and len(sizes) % RING == 0 and len(sizes) % E_RING == 0
    return [(sum(sizes[:c]), n) for c, n in enumerate(sizes)]


def groups_of(tiles):
    sizes = [3] * 8 + [2]
    assert sum(sizes) == tiles and 2 * len(sizes) % RING == 0
    return [(sum(sizes[:g]), n) for g, n in enumerate(sizes)]


def adj_resnorm_kernel(nc, x, adj_t, w_sa, w_sa_t, a_sa, w_gcnb, b_gcnb, wa, ba, wb, bb, out):
    TILES, _, D = x.shape
    KT = D // P
    CHUNKS = chunks_of(TILES)
    NC = len(CHUNKS)
    GROUPS = groups_of(TILES)
    EARLY = 2 * len(GROUPS)
    LAST = TILES - 1
    HALVES = [slice(0, D // 2), slice(D // 2, D)]
    assert TILES % 2 == 0

    with ExitStack() as ctx:
        def sb(name, shape, dt=F32):
            return ctx.enter_context(nc.sbuf_tensor(name, shape, dt))

        def psum(name, shape):
            return ctx.enter_context(nc.psum_tensor(name, shape, F32))

        def sem(name):
            return ctx.enter_context(nc.semaphore(name))

        x_hi = sb("x_hi", [P, TILES, D], F32R)
        x_lo = sb("x_lo", [P, TILES, D], F32R)
        w_hi = sb("w_hi", [P, 2, KT, D], F32R)
        w_lo = sb("w_lo", [P, 2, KT, D], F32R)
        width = [CHUNKS[s][1] for s in range(RING)]
        adj = [sb(f"adj{s}", [P, width[s], P]) for s in range(RING)]
        adj_r = [sb(f"adj_r{s}", [P, width[s], P], F32R) for s in range(RING)]
        e_hi = [sb(f"e_hi{s}", [P, width[s], P], F32R) for s in range(RING)]
        e_lo = [sb(f"e_lo{s}", [P, width[s], P], F32R) for s in range(RING)]
        e_raw = [sb(f"e_raw{s}", [P, max(width), P]) for s in range(E_RING)]
        esums = sb("esums", [P, NC + 2, P])
        esum = esums[:, 0:NC, :]
        esum_all = esums[:, NC:NC + 2, :]
        zt_hi = sb("zt_hi", [P, 2, D], F32R)
        zt_lo = sb("zt_lo", [P, 2, D], F32R)
        work = sb("work", [P, 4, D])
        zs = work[:, 0:2, :]
        y = [work[:, 2, :], work[:, 3, :]]
        x_row = sb("x_row", [P, D])
        first_adj = work[:, 2:4, :].rearrange("p n d -> p (n d)")[:, 0:CHUNKS[0][1] * P] \
            .rearrange("p (j i) -> p j i", i=P)
        product = sb("product", [P, 2, D], BF16)
        w_t = [e_raw[n][:, 0:KT, :].rearrange("p k i -> p (k i)") for n in range(E_RING)]
        w_t += [esums[:, n * KT:(n + 1) * KT, :].rearrange("p k i -> p (k i)") for n in range(2)]
        v_l = sb("v_l", [P, D])
        v_r = sb("v_r", [P, D])[:, :]
        work_a = [v[:, :].rearrange("p (k m) -> p k m", k=KT) for v in (v_l, x_row)]
        w_gate = sb("w_gate", [P, 2, 2, D])
        stage = [work[:, n, :] for n in range(4)] + [w_gate[:, n // 2, n % 2, :] for n in range(4)]
        bias_row = v_r
        ident = sb("ident", [P, P])
        ones = sb("ones", [P, P])
        diag = sb("diag", [P, P])
        l_row = sb("l_row", [P, 2, P])
        r_col = sb("r_col", [P, TILES])
        r_neg = sb("r_neg", [P, TILES])
        a_col = sb("a_col", [P, 2, KT])
        gate_bias = sb("gate_bias", [P, 2])
        row_cols = sb("row_cols", [P, 2, 3])
        held_cols = sb("held_cols", [P, 3])
        gate_z = sb("gate_z", [P, 2])
        denom = sb("denom", [P, 2, 4])
        gates = sb("gates", [P, 2, 2])
        inverse = sb("inverse", [P, 2])
        row_w = sb("row_w", [P, 2])
        alpha = sb("alpha", [P, 2])
        stats = sb("stats", [P, 2, 6])
        factor = sb("factor", [P, 8])
        scratch = sb("scratch", [P, 16])
        norm = sb("norm", [P, 2, 3])

        z1 = [psum(f"z1_{n}", [P, D]) for n in range(2)]
        z2 = [psum(f"z2_{n}", [P, D]) for n in range(2)]
        zt = [psum(f"zt_{n}", [P, D]) for n in range(2)]
        proj = psum("proj", [P, D])
        misc = psum("misc", [P, D])
        proj_half = [proj[:, 0:D // 2], z2[0][:, 0:D // 2]]
        l_psum = misc[:, 0:P]
        den_psum = misc[:, P:P + 1]

        x_staged = [sem(f"x_staged{n}") for n in range(STAGES)]
        w_staged = [sem(f"w_staged{n}") for n in range(4)]
        vectors = sem("vectors")
        a_loaded = sem("a_loaded")
        w_t_loaded = [sem(f"w_t_loaded{k}") for k in range(KT)]
        bias_loaded = sem("bias_loaded")
        first_loaded = sem("first_loaded")
        adj_loaded = [sem(f"adj_loaded{s}") for s in range(RING)]
        stored = [sem(f"stored{n}") for n in range(2)]
        ident_zero, ident_ready = sem("ident_zero"), sem("ident_ready")
        ones_ready = sem("ones_ready")
        a_spread, v_summed, v_ready = sem("a_spread"), sem("v_summed"), sem("v_ready")
        w_hi_ready, w_lo_ready = sem("w_hi_ready"), sem("w_lo_ready")
        x_hi_ready, r_dot, r_ready, x_lo_ready = sem("x_hi_ready"), sem("r_dot"), sem("r_ready"), sem("x_lo_ready")
        x_lo_shared = sem("x_lo_shared")
        bias_neg = sem("bias_neg")
        cols_held = sem("cols_held")
        row_joined, row_dots, diag_ready = sem("row_joined"), sem("row_dots"), sem("diag_ready")
        l_spread, l_ready = sem("l_spread"), sem("l_ready")
        relu_done, exp_done = sem("relu_done"), sem("exp_done")
        adj_r_ready, adj_r_second = sem("adj_r_ready"), sem("adj_r_second")
        masked, e_hi_ready, e_lo_ready = sem("masked"), sem("e_hi_ready"), sem("e_lo_ready")
        esum_ready, esum_all_ready = sem("esum_ready"), sem("esum_all_ready")
        adj_r_used, parts_used, den_ready = sem("adj_r_used"), sem("parts_used"), sem("den_ready")
        z_dots, gate_exp = sem("z_dots"), sem("gate_exp")
        gate_denoms, gates_ready = sem("gate_denoms"), sem("gates_ready")
        denoms, inverses, alpha_ready, zs_ready = sem("denoms"), sem("inverses"), sem("alpha_ready"), sem("zs_ready")
        zt_ready, zt_hi_ready, zt_lo_ready = sem("zt_ready"), sem("zt_hi_ready"), sem("zt_lo_ready")
        proj_ready, u_ready, tanh_ready = sem("proj_ready"), sem("u_ready"), sem("tanh_ready")
        y_steps, stats_ready = sem("y_steps"), sem("stats_ready")
        row_raised, last_steps = sem("row_raised"), sem("last_steps")
        factor_ready, moment_steps, norm_ready, y_ready = (sem(n) for n in ("factor_ready", "moment_steps",
                                                                            "norm_ready", "y_ready"))

        block = ctx.enter_context(nc.Block())

        def since(eng, s, value):
            if not isinstance(value, int) or value > 0:
                eng.wait_ge(s, value)

        def for_tiles(eng, tile):
            for t in range(2):
                tile(t, t)
            with eng.Fori(1, TILES // 2 - 1) as pair:
                tile(pair * 2, 0)
                tile(pair * 2 + 1, 1)
            tile(LAST - 1, 0)

        def shared(jt):
            return jt % 3 < 2

        def shared_before(jt):
            return sum(shared(n) for n in range(jt))

        def copied(t, c):
            return t * NC + (EARLY - 2 * NC + c)

        def copies_before(t, c):
            return copied(t, c) - len(GROUPS)

        def early_copied(eng, number):
            eng.wait_ge((adj_r_ready, adj_r_second)[number % 2], number // 2 + 1)

        def copy_early(eng, copy, number):
            n = GROUPS[number // 2][1]
            eng.wait_ge(adj_loaded[number % RING], (number // RING + 1) * 16)
            since(eng, adj_r_used, number - RING + 1)
            copy(adj_r[number % RING][:, 0:n, :], adj[number % RING][:, 0:n, :]) \
                .then_inc((adj_r_ready, adj_r_second)[number % 2], 1)

        def adj_landed(eng, base, c):
            eng.wait_ge(adj_loaded[c % RING], base + (c // RING + (0 if c % RING == 0 else 1)) * 16)

        def loads_before(t, again=True):
            return t * (NC // RING * 16) + (EARLY // RING + (NC // RING if last(t) and again else 0)) * 16

        def first(t):
            return isinstance(t, int) and t == 0

        def second(t):
            return isinstance(t, int) and t == 1

        def last(t):
            return isinstance(t, int) and t == LAST

        def has_older(t):
            return not isinstance(t, int) or t >= 2

        def x_rows(t):
            if isinstance(t, int):
                return x_hi[:, t, :].bitcast(F32), x_lo[:, t, :].bitcast(F32)
            return tuple(v[:, bass.ds(t, 1), :].rearrange("p o d -> p (o d)").bitcast(F32) for v in (x_hi, x_lo))

        @block.sync
        def _(sp):
            def x_split(jt):
                sp.wait_ge(r_dot, jt + 1)
                if shared(jt):
                    sp.wait_ge(x_lo_shared, shared_before(jt + 1))
                else:
                    sp.wait_ge(x_lo_ready, jt + 1 - shared_before(jt + 1))

            def load_x(g):
                for jt in range(GROUPS[g][0], sum(GROUPS[g])):
                    if jt >= STAGES:
                        x_split(jt - STAGES)
                    sp.dma_start(stage[jt % STAGES], x[jt]).then_inc(x_staged[jt % STAGES], 16)

            def load_w(n):
                if n < 4:
                    if n >= 2:
                        sp.wait_ge(masked, 1)
                    x_split(TILES - 1 - (TILES - 1 - n) % STAGES)
                else:
                    sp.wait_ge(w_lo_ready, n - 3)
                sp.dma_start(stage[n % 4], (w_sa, w_gcnb)[n // KT][n % KT]).then_inc(w_staged[n % 4], 16)

            def load_vectors():
                for n in range(4, STAGES):
                    x_split(TILES - 1 - (TILES - 1 - n) % STAGES)
                for g, w in enumerate((wa, wb)):
                    sp.dma_start(w_gate[:, g, :, :].rearrange("p h d -> p (h d)"),
                                 w.to_broadcast([P, 2 * D])).then_inc(vectors, 16)
                for g, b in enumerate((ba, bb)):
                    sp.dma_start(gate_bias[:, g:g + 1], b.to_broadcast([P, 1])).then_inc(vectors, 16)

            def load_early(number):
                g, t = number // 2, number % 2
                j, n = GROUPS[g]
                if number >= RING:
                    early_copied(sp, number - RING)
                sp.dma_start(adj[number % RING][:, 0:n, :], adj_t[t, :, j:j + n, :]) \
                    .then_inc(adj_loaded[number % RING], 16)

            def load_first_chunk():
                for n in (2, 3):
                    x_split(TILES - 1 - (TILES - 1 - n) % STAGES)
                sp.dma_start(first_adj, adj_t[0, :, 0:CHUNKS[0][1], :]).then_inc(first_loaded, 16)

            def load_adj(t, c, copies, masks):
                j, n = CHUNKS[c]
                since(sp, adj_r_ready, copies)
                since(sp, masked, masks)
                sp.dma_start(adj[c % RING][:, :, :], adj_t[t, :, j:j + n, :]).then_inc(adj_loaded[c % RING], 16)

            def store(t, parity):
                sp.wait_ge(y_ready, t + 1)
                sp.dma_start(out[t], y[parity]).then_inc(stored[parity], 16)

            sp.dma_start(a_col[:, :, :], a_sa).then_inc(a_loaded, 16)
            for k in range(KT):
                sp.dma_start(w_t[k], w_sa_t[k]).then_inc(w_t_loaded[k], 16)
            load_x(0)
            for number in range(RING):
                load_early(number)
            for g in range(1, AHEAD + 1):
                load_x(g)
            for g in range(1, len(GROUPS)):
                if g == len(GROUPS) - 1:
                    load_first_chunk()
                load_early(2 * g + 1)
                if g + AHEAD < len(GROUPS):
                    load_x(g + AHEAD)
                if 2 * g + 2 < EARLY:
                    load_early(2 * g + 2)

            def tile(t, parity):
                for c in range(NC):
                    if first(t) and 1 <= c <= RING:
                        early_copied(sp, EARLY - RING + c % RING)
                    if first(t) and c == 0:
                        load_vectors()
                    else:
                        load_adj(t, c, 0, t * NC + (c - RING + 1))
                    if first(t) and c == 2:
                        for n in range(4):
                            load_w(n)
                    if second(t) and c < 4:
                        load_w(4 + c)
                if first(t):
                    sp.wait_ge(r_dot, TILES)
                    sp.dma_start(bias_row, b_gcnb.to_broadcast([P, D])).then_inc(bias_loaded, 16)
                if has_older(t):
                    store(t - 2, parity)

            for_tiles(sp, tile)
            for c in range(NC):
                load_adj(LAST, c, copies_before(LAST, c) - (RING - 1), LAST * NC + min(c - RING + 1, 0))
            for c in range(NC):
                load_adj(LAST, c, copies_before(LAST, NC), LAST * NC + (c - RING + 1))
            store(LAST - 2, 1)
            store(LAST - 1, 0)
            for n, half in enumerate(HALVES):
                sp.wait_ge(y_ready, LAST + 1 + n)
                sp.dma_start(out[LAST, :, half], y[1][:, half]).then_inc(stored[1], 16)
            for n in range(2):
                sp.wait_ge(stored[n], 16 * (TILES // 2 + n))

        @block.gpsimd
        def _(pool):
            nc.gpsimd.memset(ident[:, :], 0.0).then_inc(ident_zero, 1)
            pool.wait_ge(ident_zero, 1)
            nc.gpsimd.affine_select(out=ident[:, :], in_=ident[:, :], compare_op=ALU.not_equal, fill=1.0, base=0,
                                    pattern=[[-1, P]], channel_multiplier=1).then_inc(ident_ready, 1)
            nc.gpsimd.memset(ones[:, :], 1.0).then_inc(ones_ready, 1)
            for n, value in enumerate((0.5, 1.0 / D, 0.25, EPS_NORM, -0.5, 1.5)):
                nc.gpsimd.memset(factor[:, n:n + 1], value).then_inc(factor_ready, 1)
            pool.wait_ge(factor_ready, 6)

            for jt in filter(shared, range(TILES)):
                pool.wait_ge(x_hi_ready, jt + 1)
                pool.wait_ge(x_staged[jt % STAGES], 16 * (jt // STAGES + 1))
                nc.gpsimd.tensor_tensor(x_lo[:, jt, :], stage[jt % STAGES], x_hi[:, jt, :].bitcast(F32),
                                        ALU.subtract).then_inc(x_lo_shared, 1)

            for n in range(2 * KT):
                m, k = n // KT, n % KT
                pool.wait_ge(w_staged[n % 4], 16 * (n // 4 + 1))
                nc.gpsimd.tensor_copy(w_hi[:, m, k, :], stage[n % 4]).then_inc(w_hi_ready, 1)
                pool.wait_ge(w_hi_ready, n + 1)
                nc.gpsimd.tensor_tensor(w_lo[:, m, k, :], stage[n % 4], w_hi[:, m, k, :].bitcast(F32),
                                        ALU.subtract).then_inc(w_lo_ready, 1)

            def moments(t, parity):
                s, m = stats[:, parity, :], scratch
                pool.wait_ge(stats_ready, t + 1)
                steps = [
                    (m[:, 0:2], s[:, 1:3], s[:, 4:6], ALU.add),
                    (m[:, 2:3], s[:, 1:2], s[:, 4:5], ALU.subtract),
                    (m[:, 3:4], m[:, 2:3], m[:, 2:3], ALU.mult),
                    (norm[:, parity, 0:2], m[:, 0:2], factor[:, 0:2], ALU.mult),
                    (m[:, 6:7], m[:, 3:4], factor[:, 2:3], ALU.mult),
                    (m[:, 7:8], norm[:, parity, 1:2], m[:, 6:7], ALU.add),
                    (m[:, 8:9], m[:, 7:8], factor[:, 3:4], ALU.add),
                    (m[:, 9:10], m[:, 8:9], factor[:, 4:5], ALU.pow),
                    (m[:, 10:11], m[:, 9:10], m[:, 9:10], ALU.mult),
                    (m[:, 11:12], m[:, 10:11], m[:, 8:9], ALU.mult),
                    (m[:, 12:13], m[:, 11:12], factor[:, 4:5], ALU.mult),
                    (m[:, 13:14], m[:, 12:13], factor[:, 5:6], ALU.add),
                    (norm[:, parity, 2:3], m[:, 13:14], m[:, 9:10], ALU.mult),
                ]
                for n, (dst, a, b, op) in enumerate(steps):
                    if n:
                        pool.wait_ge(moment_steps, t * (len(steps) - 1) + n)
                    ins = nc.gpsimd.tensor_tensor(dst, a, b, op)
                    ins.then_inc(moment_steps if n < len(steps) - 1 else norm_ready, 1)

            for_tiles(pool, moments)
            pool.wait_ge(last_steps, 2)
            nc.gpsimd.tensor_tensor(scratch[:, 3:4], scratch[:, 2:3], factor[:, 4:5], ALU.pow) \
                .then_inc(last_steps, 1)

        @block.scalar
        def _(act):
            def x_part(jt):
                act.wait_ge(x_staged[jt % STAGES], 16 * (jt // STAGES + 1))
                nc.scalar.copy(x_hi[:, jt, :], stage[jt % STAGES]).then_inc(x_hi_ready, 1)

            def weights(t, parity, c):
                j, n = CHUNKS[c]
                e = e_raw[c % E_RING]
                if c == 0:
                    act.wait_ge(l_ready, t + 1)
                if first(t):
                    act.wait_ge(r_ready, j + n)
                since(act, e_lo_ready, t * NC + (c - E_RING + 1))
                for k in range(n):
                    ins = nc.scalar.activation(e[:, k, :], l_row[:, parity, :], ACT.Relu,
                                                bias=r_col[:, j + k:j + k + 1])
                ins.then_inc(relu_done, 1)
                act.wait_ge(relu_done, t * NC + (c + 1))
                for k in range(n):
                    ins = nc.scalar.activation(e[:, k, :], e[:, k, :], ACT.Exp, scale=SLOPE - 1.0,
                                                bias=r_neg[:, j + k:j + k + 1])
                ins.then_inc(exp_done, 1)

            def adjacency(t, c):
                adj_landed(act, loads_before(t, again=False), c)
                act.wait_ge(adj_r_used, copied(t, c) - (RING - 1))
                nc.scalar.copy(adj_r[c % RING][:, :, :], adj[c % RING][:, :, :]).then_inc(adj_r_ready, 1)

            def gate_exps(t, parity):
                act.wait_ge(z_dots, t * 2 + 2)
                act.wait_ge(cols_held, t + 1)
                for g in range(2):
                    nc.scalar.activation(denom[:, parity, g:g + 1], gate_z[:, g:g + 1], ACT.Exp, scale=-1.0,
                                         bias=held_cols[:, g:g + 1])
                nc.scalar.activation(row_w[:, parity:parity + 1], held_cols[:, 2:3], ACT.Exp,
                                     scale=-SLOPE).then_inc(gate_exp, 1)

            def zt_part(t, h):
                act.wait_ge(zt_ready, t * 2 + (2 - h))
                since(act, proj_ready, t * 2 - h)
                nc.scalar.copy(zt_hi[:, h, :], zt[h][:, :]).then_inc(zt_hi_ready, 1)

            def tanh_half(t, parity):
                act.wait_ge(u_ready, t + 1)
                nc.scalar.activation(y[parity], y[parity], ACT.Tanh, scale=0.5).then_inc(tanh_ready, 1)

            for jt in range(GROUPS[0][1]):
                x_part(jt)
            act.wait_ge(v_summed, KT)
            nc.scalar.copy(v_r, zt[1][:, :]).then_inc(v_ready, 1)
            for g in range(len(GROUPS)):
                if g == 0:
                    copy_early(act, nc.scalar.copy, 0)
                if g + 1 < len(GROUPS):
                    for jt in range(GROUPS[g + 1][0], sum(GROUPS[g + 1])):
                        x_part(jt)
                if g > 0:
                    copy_early(act, nc.scalar.copy, 2 * g)
                if g == 1:
                    act.wait_ge(v_summed, 2 * KT)
                    nc.scalar.copy(v_l[:, :], zt[0][:, :]).then_inc(v_ready, 1)
                if g == 5:
                    weights(0, 0, 0)
                if g == 7:
                    weights(0, 0, 1)

            def tile(t, parity):
                for c in range(NC):
                    if not (first(t) and c < 2):
                        weights(t, parity, c)
                    if has_older(t):
                        adjacency(t, c)
                    if c == 3 and not first(t):
                        gate_exps(t - 1, 1 - parity)
                        if has_older(t):
                            tanh_half(t - 2, parity)
                    if c == 5 and not first(t):
                        zt_part(t - 1, 1)
                        zt_part(t - 1, 0)

            for_tiles(act, tile)
            for c in range(NC):
                adjacency(LAST, c)
                if c < 2:
                    weights(LAST, 1, c)
                if c == 2:
                    gate_exps(LAST - 1, 0)
                    tanh_half(LAST - 2, 1)
            zt_part(LAST - 1, 1)
            zt_part(LAST - 1, 0)
            weights(LAST, 1, 2)
            weights(LAST, 1, 3)
            gate_exps(LAST, 1)
            weights(LAST, 1, 4)
            weights(LAST, 1, 5)
            zt_part(LAST, 1)
            tanh_half(LAST - 1, 0)
            zt_part(LAST, 0)
            for n, half in enumerate(HALVES):
                act.wait_ge(u_ready, LAST + 1 + n)
                nc.scalar.activation(y[1][:, half], y[1][:, half], ACT.Tanh, scale=0.5).then_inc(tanh_ready, 1)

        @block.tensor
        def _(pe):
            def sum_v():
                for h in (1, 0):
                    for k in range(KT):
                        pe.wait_ge(a_spread, (1 - h) * KT + k + 1)
                        pe.wait_ge(w_t_loaded[k], 16)
                        nc.tensor.matmul(zt[h][:, :], work_a[h][:, k, :], w_t[k], start=(k == 0),
                                         stop=(k == KT - 1)).then_inc(v_summed, 1)

            def spread_l(t):
                pe.wait_ge(diag_ready, t + 1)
                nc.tensor.matmul(l_psum, ones[:, :], diag[:, :], start=True, stop=True).then_inc(l_spread, 1)

            def sum_z2(buffer, parity, j, n):
                for k in range(n):
                    jt = j + k
                    nc.tensor.matmul(z2[parity][:, :], buffer[:, k, :], x_hi[:, jt, :], start=(jt == 0), stop=False)
                    ins = nc.tensor.matmul(z2[parity][:, :], buffer[:, k, :], x_lo[:, jt, :], start=False,
                                           stop=(jt == TILES - 1))
                ins.then_inc(adj_r_used, 1)

            def early(g, t):
                j, n = GROUPS[g]
                number = 2 * g + t
                early_copied(pe, number)
                pe.wait_ge(x_lo_shared, shared_before(j + n))
                pe.wait_ge(x_lo_ready, j + n - shared_before(j + n))
                sum_z2(adj_r[number % RING], t, j, n)

            def chunk_z2(t, parity, c):
                pe.wait_ge(adj_r_ready, copies_before(t, c) + 1)
                if c == 0:
                    pe.wait_ge(zs_ready, t * 2 - 2)
                sum_z2(adj_r[c % RING], parity, *CHUNKS[c])

            def chunk_z1(t, parity, c):
                j, n = CHUNKS[c]
                s = c % RING
                pe.wait_ge(e_lo_ready, t * NC + (c + 1))
                for k in range(n):
                    jt = j + k
                    nc.tensor.matmul(z1[parity][:, :], e_hi[s][:, k, :], x_hi[:, jt, :], start=(jt == 0), stop=False)
                    nc.tensor.matmul(z1[parity][:, :], e_hi[s][:, k, :], x_lo[:, jt, :], start=False, stop=False)
                    ins = nc.tensor.matmul(z1[parity][:, :], e_lo[s][:, k, :], x_hi[:, jt, :], start=False,
                                           stop=(jt == TILES - 1))
                ins.then_inc(parts_used, 1)

            def denominator(t, parity):
                pe.wait_ge(esum_all_ready, t + 1)
                if last(t):
                    pe.wait_ge(esum_ready, LAST * NC + NC)
                pe.wait_ge(l_ready, TILES if last(t) else t + 2)
                since(pe, denoms, t)
                ins = nc.tensor.matmul(den_psum, esum_all[:, parity, :], ones[:, 0:1], start=True, stop=not last(t))
                if last(t):
                    ins = nc.tensor.matmul(den_psum, esum[:, NC - 1, :], ones[:, 0:1], start=False, stop=True)
                ins.then_inc(den_ready, 1)

            def turn(t, h):
                pe.wait_ge(zs_ready, t * 2 + (2 - h))
                since(pe, zt_lo_ready, t * 2 - h)
                for k in range(KT):
                    ins = nc.tensor.transpose(zt[h][:, k * P:(k + 1) * P], zs[:, h, k * P:(k + 1) * P], ident[:, :])
                ins.then_inc(zt_ready, 1)

            def project(t, h):
                pe.wait_ge(zt_lo_ready, t * 2 + (2 - h))
                if h == 1:
                    if first(t):
                        pe.wait_ge(w_lo_ready, 2 * KT)
                    since(pe, u_ready, t)
                for k in range(KT):
                    for a, b in ((zt_hi, w_hi), (zt_hi, w_lo), (zt_lo, w_hi)):
                        ins = nc.tensor.matmul(proj[:, :], a[:, h, k * P:(k + 1) * P], b[:, h, k, :],
                                               start=(h == 1 and k == 0 and a is zt_hi and b is w_hi),
                                               stop=(h == 0 and k == KT - 1 and a is zt_lo))
                ins.then_inc(proj_ready, 1)

            def project_halves(h):
                pe.wait_ge(zt_lo_ready, LAST * 2 + (2 - h))
                if h == 1:
                    pe.wait_ge(u_ready, LAST)
                for n, half in enumerate(HALVES):
                    for k in range(KT):
                        for a, b in ((zt_hi, w_hi), (zt_hi, w_lo), (zt_lo, w_hi)):
                            ins = nc.tensor.matmul(proj_half[n], a[:, h, k * P:(k + 1) * P], b[:, h, k, half],
                                                   start=(h == 1 and k == 0 and a is zt_hi and b is w_hi),
                                                   stop=(h == 0 and k == KT - 1 and a is zt_lo))
                    if h == 0:
                        ins.then_inc(proj_ready, 1)

            sum_v()
            for g in range(len(GROUPS)):
                for t in range(2):
                    early(g, t)
                if g == 2:
                    spread_l(0)

            def tile(t, parity):
                for c in range(NC):
                    if has_older(t):
                        chunk_z2(t, parity, c)
                    chunk_z1(t, parity, c)
                    if c == (2 if first(t) else 0):
                        since(pe, denoms, t - 1)
                        spread_l(t + 1)
                    if c == (3 if second(t) else 2) and not first(t):
                        turn(t - 1, 1)
                        turn(t - 1, 0)
                    if c == 4 and not first(t):
                        project(t - 1, 1)
                        project(t - 1, 0)
                denominator(t, parity)

            pe.wait_ge(ident_ready, 1)
            for_tiles(pe, tile)
            for c in range(NC):
                chunk_z2(LAST, 1, c)
                if c == 2:
                    turn(LAST - 1, 1)
                    turn(LAST - 1, 0)
            chunk_z1(LAST, 1, 0)
            project(LAST - 1, 1)
            project(LAST - 1, 0)
            for c in range(1, NC):
                chunk_z1(LAST, 1, c)
                if c == 4:
                    turn(LAST, 1)
            denominator(LAST, 1)
            project_halves(1)
            turn(LAST, 0)
            project_halves(0)

        @block.vector
        def _(dve):
            def dot(in0, in1, scale, start, accum, done, count, turn):
                since(dve, done, count - 1)
                nc.vector.tensor_tensor_reduce(product[:, turn, :], in0, in1, scale, start, ALU.mult, ALU.add,
                                               accum).then_inc(done, 1)

            dve.wait_ge(a_loaded, 16)
            dve.wait_ge(ones_ready, 1)
            for h in (1, 0):
                for k in range(KT):
                    nc.vector.tensor_scalar(work_a[h][:, k, :], ones[:, :], a_col[:, h, k:k + 1], None, ALU.mult) \
                        .then_inc(a_spread, 1)
            def sources(g):
                j, n = GROUPS[g]
                for jt in range(j, j + n):
                    dve.wait_ge(x_staged[jt % STAGES], 16 * (jt // STAGES + 1))
                    dot(stage[jt % STAGES], v_r, 1.0, 0.0, r_col[:, jt:jt + 1], r_dot, jt, jt % 2)
                    if not shared(jt):
                        dve.wait_ge(x_hi_ready, jt + 1)
                        nc.vector.tensor_tensor(x_lo[:, jt, :], stage[jt % STAGES], x_hi[:, jt, :].bitcast(F32),
                                                ALU.subtract).then_inc(x_lo_ready, 1)
                    if jt == j and g > 0:
                        negate_r(g - 1)

            def negate_r(g):
                j, n = GROUPS[g]
                dve.wait_ge(r_dot, j + n)
                nc.vector.tensor_scalar(r_neg[:, j:j + n], r_col[:, j:j + n], -SLOPE, None, ALU.mult) \
                    .then_inc(r_ready, n)

            def target_l(t, parity):
                hi, lo = x_rows(t)
                since(dve, row_dots, t * 3)
                nc.vector.tensor_tensor(x_row[:, :], hi, lo, ALU.add).then_inc(row_joined, 1)
                dve.wait_ge(row_joined, t + 1)
                dot(x_row[:, :], v_l[:, :], 1.0, 0.0, row_cols[:, parity, 2:3], row_dots, t * 3, 0)
                since(dve, l_spread, t)
                dve.wait_ge(row_dots, t * 3 + 1)
                nc.vector.tensor_scalar(diag[:, :], ident[:, :], row_cols[:, parity, 2:3], None, ALU.mult) \
                    .then_inc(diag_ready, 1)

            def target_gates(t, parity):
                for g in range(2):
                    dot(x_row[:, :], w_gate[:, g, 1, :], -1.0, gate_bias[:, g:g + 1], row_cols[:, parity, g:g + 1],
                        row_dots, t * 3 + (g + 1), 1 - g)

            def hold_cols(t, parity):
                nc.vector.tensor_copy(held_cols[:, :], row_cols[:, parity, :]).then_inc(cols_held, 1)

            def l_copy(t, parity):
                dve.wait_ge(l_spread, t + 1)
                nc.vector.tensor_copy(l_row[:, parity, :], l_psum).then_inc(l_ready, 1)

            def parts(t, parity, c):
                n = CHUNKS[c][1]
                s = c % RING
                e = e_raw[c % E_RING][:, 0:n, :]
                count = t * NC + (c + 1)
                dve.wait_ge(exp_done, count)
                if first(t) and c == 0:
                    mask = first_adj
                    dve.wait_ge(first_loaded, 16)
                else:
                    mask = adj[s][:, :, :]
                    adj_landed(dve, loads_before(t), c)
                if has_older(t) and not last(t):
                    dve.wait_ge(adj_r_ready, copies_before(t, c) + 1)
                nc.vector.scalar_tensor_tensor(e, mask, 0.0, e, ALU.not_equal, ALU.mult) \
                    .then_inc(masked, 1)
                dve.wait_ge(masked, count)
                since(dve, parts_used, t * NC + (c - RING + 1))
                nc.vector.tensor_copy(e_hi[s][:, :, :], e).then_inc(e_hi_ready, 1)
                nc.vector.tensor_reduce(esum[:, c, :], e.rearrange("p j i -> p i j"), AX_X, ALU.add) \
                    .then_inc(esum_ready, 1)
                dve.wait_ge(e_hi_ready, count)
                nc.vector.tensor_tensor(e_lo[s][:, :, :], e, e_hi[s][:, :, :].bitcast(F32), ALU.subtract) \
                    .then_inc(e_lo_ready, 1)

            def join_esum(t, parity):
                n = NC - 1 if last(t) else NC
                dve.wait_ge(esum_ready, t * NC + n)
                since(dve, den_ready, t - 1)
                nc.vector.tensor_reduce(esum_all[:, parity, :], esum[:, 0:n, :].rearrange("p c i -> p i c"), AX_X,
                                        ALU.add).then_inc(esum_all_ready, 1)

            def gate_dots(t, parity):
                if last(t):
                    dve.wait_ge(adj_r_used, copied(LAST, NC))
                else:
                    dve.wait_ge(parts_used, t * NC + NC)
                for g in range(2):
                    dot(z2[parity][:, :], w_gate[:, g, 0, :], 1.0, 0.0, gate_z[:, g:g + 1], z_dots, t * 2 + g, g)

            def scale_z2(t, parity):
                dve.wait_ge(gate_exp, t + 1)
                nc.vector.tensor_scalar(denom[:, parity, 0:2], denom[:, parity, 0:2], 1.0, None, ALU.add) \
                    .then_inc(gate_denoms, 1)
                dve.wait_ge(gate_denoms, t + 1)
                nc.vector.reciprocal(gates[:, parity, :], denom[:, parity, 0:2]).then_inc(gates_ready, 1)
                dve.wait_ge(gates_ready, t + 1)
                if first(t):
                    dve.wait_ge(w_lo_ready, 2 * KT)
                    dve.wait_ge(bias_loaded, 16)
                since(dve, zt_ready, t * 2)
                nc.vector.tensor_scalar(zs[:, 1, :], z2[parity][:, :], gates[:, parity, 1:2], None, ALU.mult) \
                    .then_inc(zs_ready, 1)

            def scale_z1(t, parity):
                dve.wait_ge(den_ready, t + 1)
                nc.vector.tensor_scalar(denom[:, parity, 2:3], den_psum, row_w[:, parity:parity + 1], EPS_ATTN,
                                        ALU.mult, ALU.add).then_inc(denoms, 1)
                dve.wait_ge(denoms, t + 1)
                nc.vector.reciprocal(inverse[:, parity:parity + 1], denom[:, parity, 2:3]).then_inc(inverses, 1)
                dve.wait_ge(inverses, t + 1)
                nc.vector.scalar_tensor_tensor(alpha[:, parity:parity + 1], gates[:, parity, 0:1],
                                               row_w[:, parity:parity + 1], inverse[:, parity:parity + 1], ALU.mult,
                                               ALU.mult).then_inc(alpha_ready, 1)
                dve.wait_ge(alpha_ready, t + 1)
                nc.vector.tensor_scalar(zs[:, 0, :], z1[parity][:, :], alpha[:, parity:parity + 1], None, ALU.mult) \
                    .then_inc(zs_ready, 1)

            def zt_rest(t, h):
                dve.wait_ge(zt_hi_ready, t * 2 + (2 - h))
                since(dve, proj_ready, t * 2 - h)
                nc.vector.tensor_tensor(zt_lo[:, h, :], zt[h][:, :], zt_hi[:, h, :].bitcast(F32),
                                        ALU.subtract).then_inc(zt_lo_ready, 1)

            def add_bias(t, parity):
                dve.wait_ge(proj_ready, t * 2 + 2)
                if has_older(t):
                    dve.wait_ge(stored[parity], (t - parity) * 8)
                nc.vector.scalar_tensor_tensor(y[parity], bias_row, gates[:, parity, 1:2], proj[:, :],
                                               ALU.mult, ALU.add).then_inc(u_ready, 1)

            def residual(t, parity):
                hi, lo = x_rows(t)
                dve.wait_ge(tanh_ready, t + 1)
                nc.vector.scalar_tensor_tensor(y[parity], y[parity], 0.5, lo, ALU.mult, ALU.add).then_inc(y_steps, 1)
                dve.wait_ge(y_steps, t * 2 + 1)
                nc.vector.scalar_tensor_tensor(y[parity], y[parity], 0.5, hi, ALU.add, ALU.add).then_inc(y_steps, 1)
                dve.wait_ge(y_steps, t * 2 + 2)
                nc.vector.bn_stats(stats[:, parity, :], y[parity]).then_inc(stats_ready, 1)

            def normalise(t, parity):
                dve.wait_ge(norm_ready, t + 1)
                nc.vector.tensor_scalar(y[parity], y[parity], norm[:, parity, 0:1], norm[:, parity, 2:3],
                                        ALU.subtract, ALU.mult).then_inc(y_ready, 1)

            dve.wait_ge(v_ready, 1)
            for g in range(len(GROUPS)):
                sources(g)
                if g < len(GROUPS) - 2:
                    copy_early(dve, nc.vector.tensor_copy, 2 * g + 1)
                if g == len(GROUPS) - 1:
                    copy_early(dve, nc.vector.tensor_copy, 2 * g - 1)
                if g == 2:
                    dve.wait_ge(ident_ready, 1)
                    dve.wait_ge(v_ready, 2)
                    dve.wait_ge(x_lo_shared, 1)
                    target_l(0, 0)
                if g == 4:
                    l_copy(0, 0)

            def tile(t, parity):
                for c in range(NC):
                    if not (first(t) and c == 0):
                        parts(t, parity, c)
                    if first(t):
                        if c == 1:
                            dve.wait_ge(vectors, 16 * 4)
                            nc.vector.tensor_scalar(gate_bias[:, :], gate_bias[:, :], -1.0, None, ALU.mult) \
                                .then_inc(bias_neg, 1)
                            dve.wait_ge(bias_neg, 1)
                            target_gates(0, 0)
                        if c == 2:
                            target_l(1, 1)
                        if c == 5:
                            target_gates(1, 1)
                    elif c == 0:
                        hold_cols(t - 1, 1 - parity)
                        dve.wait_ge(cols_held, t)
                        target_l(t + 1, 1 - parity)
                        target_gates(t + 1, 1 - parity)
                    if c == 2:
                        if has_older(t):
                            add_bias(t - 2, parity)
                        if not first(t):
                            gate_dots(t - 1, 1 - parity)
                    if c == 3:
                        l_copy(t + 1, 1 - parity)
                        if not first(t):
                            scale_z2(t - 1, 1 - parity)
                            scale_z1(t - 1, 1 - parity)
                    if c == 4 and has_older(t):
                        residual(t - 2, parity)
                    if c == 5:
                        if not first(t):
                            zt_rest(t - 1, 1)
                            zt_rest(t - 1, 0)
                        join_esum(t, parity)
                        if has_older(t):
                            normalise(t - 2, parity)

            negate_r(len(GROUPS) - 1)
            parts(0, 0, 0)
            copy_early(dve, nc.vector.tensor_copy, EARLY - 1)
            dve.wait_ge(x_lo_shared, shared_before(TILES))
            for_tiles(dve, tile)
            add_bias(LAST - 2, 1)
            hold_cols(LAST - 1, 0)
            gate_dots(LAST - 1, 0)
            scale_z2(LAST - 1, 0)
            scale_z1(LAST - 1, 0)
            dve.wait_ge(gate_exp, LAST)
            hold_cols(LAST, 1)
            residual(LAST - 2, 1)
            zt_rest(LAST - 1, 1)
            zt_rest(LAST - 1, 0)
            for c in range(3):
                parts(LAST, 1, c)
            normalise(LAST - 2, 1)
            dve.wait_ge(row_dots, TILES * 3)
            nc.vector.tensor_scalar(x_row[:, :], x_row[:, :], 0.5, None, ALU.add).then_inc(row_raised, 1)
            parts(LAST, 1, 3)
            gate_dots(LAST, 1)
            parts(LAST, 1, 4)
            scale_z2(LAST, 1)
            join_esum(LAST, 1)
            parts(LAST, 1, 5)
            add_bias(LAST - 1, 0)
            zt_rest(LAST, 1)
            scale_z1(LAST, 1)
            residual(LAST - 1, 0)
            zt_rest(LAST, 0)

            dve.wait_ge(stored[1], (LAST - 1) * 8)
            for n, half in enumerate(HALVES):
                dve.wait_ge(proj_ready, LAST * 2 + 1 + n)
                nc.vector.scalar_tensor_tensor(y[1][:, half], bias_row[:, half], gates[:, 1, 1:2], proj_half[n],
                                               ALU.mult, ALU.add).then_inc(u_ready, 1)
            normalise(LAST - 1, 0)
            dve.wait_ge(row_raised, 1)
            for n, half in enumerate(HALVES):
                dve.wait_ge(tanh_ready, LAST + 1 + n)
                nc.vector.scalar_tensor_tensor(y[1][:, half], y[1][:, half], 0.5, x_row[:, half], ALU.mult,
                                               ALU.add).then_inc(y_steps, 1)
                dve.wait_ge(y_steps, LAST * 2 + 1 + n)
                nc.vector.bn_stats(stats[:, n, :], y[1][:, half]).then_inc(stats_ready, 1)
            dve.wait_ge(stats_ready, LAST + 2)
            m = scratch
            nc.vector.bn_aggr(m[:, 0:2], stats[:, :, :].rearrange("p n s -> p (n s)")) \
                .then_inc(last_steps, 1)
            dve.wait_ge(last_steps, 1)
            nc.vector.tensor_scalar(m[:, 2:3], m[:, 1:2], EPS_NORM, None, ALU.add).then_inc(last_steps, 1)
            dve.wait_ge(last_steps, 3)
            nc.vector.scalar_tensor_tensor(m[:, 4:5], m[:, 3:4], m[:, 3:4], m[:, 2:3], ALU.mult,
                                           ALU.mult).then_inc(last_steps, 1)
            dve.wait_ge(last_steps, 4)
            nc.vector.tensor_scalar(m[:, 5:6], m[:, 4:5], -0.5, 1.5, ALU.mult, ALU.add).then_inc(last_steps, 1)
            dve.wait_ge(last_steps, 5)
            nc.vector.tensor_tensor(m[:, 6:7], m[:, 5:6], m[:, 3:4], ALU.mult).then_inc(last_steps, 1)
            dve.wait_ge(last_steps, 6)
            for half in HALVES:
                nc.vector.tensor_scalar(y[1][:, half], y[1][:, half], m[:, 0:1], m[:, 6:7], ALU.subtract,
                                        ALU.mult).then_inc(y_ready, 1)


def kernel(x, adj, L0_gnn_W_sa, L0_gnn_a_sa, L0_gnn_W_gcnb, L0_gnn_b_gcnb, L0_gnn_Wa, L0_gnn_ba, L0_gnn_Wb,
           L0_gnn_bb):
    import numpy as np
    import concourse.bacc as bacc
    from concourse.bass_utils import run_bass_kernel_spmd

    x = np.asarray(x)
    adj = np.asarray(adj)
    nodes, d = x.shape
    tiles = -(-nodes // P)
    x_pad = np.zeros((tiles * P, d), x.dtype)
    x_pad[:nodes] = x
    adj_pad = np.zeros((tiles * P, tiles * P), adj.dtype)
    adj_pad[:nodes, :nodes] = adj
    adj_t = adj_pad.reshape(tiles, P, tiles, P).transpose(0, 3, 2, 1)
    arrays = {
        "x": x_pad.reshape(tiles, P, d),
        "adj_t": adj_t,
        "w_sa": np.asarray(L0_gnn_W_sa).reshape(d // P, P, d),
        "w_sa_t": np.asarray(L0_gnn_W_sa).T.reshape(d // P, P, d),
        "a_sa": np.asarray(L0_gnn_a_sa).reshape(2, d // P, P).transpose(2, 0, 1),
        "w_gcnb": np.asarray(L0_gnn_W_gcnb).reshape(d // P, P, d),
        "b_gcnb": np.asarray(L0_gnn_b_gcnb).reshape(1, d),
        "wa": np.asarray(L0_gnn_Wa),
        "ba": np.asarray(L0_gnn_ba).reshape(1, 1),
        "wb": np.asarray(L0_gnn_Wb),
        "bb": np.asarray(L0_gnn_bb).reshape(1, 1),
    }
    arrays = {f"{name}_dram": np.ascontiguousarray(a) for name, a in arrays.items()}
    nc = bacc.Bacc("TRN2", target_bir_lowering=False, num_devices=1)
    args = [nc.dram_tensor(name, a.shape, mybir.dt.from_np(a.dtype), kind="ExternalInput").ap()
            for name, a in arrays.items()]
    out = nc.dram_tensor("out_dram", (tiles, P, d), F32, kind="ExternalOutput").ap()
    adj_resnorm_kernel(nc, *args, out)
    r = run_bass_kernel_spmd(nc, [arrays], core_ids=[0])
    return np.asarray(r.results[0]["out_dram"]).reshape(tiles * P, d)[:nodes]
```
